# Optimizing a Trainium2 kernel written in Bass

```python
import numpy as np
import jax
import jax.numpy as jnp

def _softmax(x, axis=-1):
    return jax.nn.softmax(x, axis=axis)

def _gelu(x):
    return jax.nn.gelu(x, approximate=True)

def _silu(x):
    return jax.nn.silu(x)

def _sigmoid(x):
    return jax.nn.sigmoid(x)

def _layernorm(x, axis=-1, eps=1e-05):
    m = jnp.mean(x, axis=axis, keepdims=True)
    v = jnp.var(x, axis=axis, keepdims=True)
    return (x - m) / jnp.sqrt(v + eps)

def _scatter_add(tgt, idx, src, axis=0):
    return tgt.at[idx].add(src)

def _segment_sum(src, seg, n):
    return jax.ops.segment_sum(src, seg, n)
kernel_name = 'mk_xattn_ffn_d4_seqx_r8_d59ff1'

def setup_inputs(seed: int=0):
    np.random.seed(seed)
    _w = jnp.asarray

    def _rec_inputs():
        import jax
        import jax.numpy as jnp
        _rk = jax.random.key(seed)
        x = -0.0002928 + 1 * jax.random.normal(jax.random.fold_in(_rk, 1), (4, 256, 128), jnp.float32)
        _lenS = 256 - jax.random.randint(jax.random.fold_in(_rk, 7), (4,), 0, max(1, 256 // 4) + 1, jnp.int32)
        _lenS2 = 64 - jax.random.randint(jax.random.fold_in(_rk, 8), (4,), 0, max(1, 64 // 4) + 1, jnp.int32)
        _ctx_1024P = jax.random.normal(jax.random.fold_in(_rk, 11), (4, 16, 128), jnp.float32)
        _ctx_1024c = jax.random.dirichlet(jax.random.fold_in(_rk, 511), 0.3 * jnp.ones((16,), jnp.float32), (4, 64))
        _ctx_1024t = jnp.einsum('bsk,bkd->bsd', _ctx_1024c, _ctx_1024P)
        _ctx_1024t = _ctx_1024t * jax.lax.rsqrt(jnp.mean(jnp.square(_ctx_1024t)) + 1e-12) * 0.953939
        ctx_1024 = -1.39393e-06 + 0.999914 * (_ctx_1024t + 0.3 * jax.random.normal(jax.random.fold_in(_rk, 611), (4, 64, 128), jnp.float32))
        fside_SxS2_0 = 0.000675642 + 1.00031 * jax.random.normal(jax.random.fold_in(_rk, 12), (256, 64), jnp.float32)
        _validS = jnp.arange(256)[None, :] < _lenS[:, None]
        _validS2 = jnp.arange(64)[None, :] < _lenS2[:, None]
        _causal = jnp.tril(jnp.ones((256, 256), dtype=bool))
        mask_BxS_bf1 = jnp.ones((4, 256), dtype=bool)
        return (x, ctx_1024, fside_SxS2_0, mask_BxS_bf1)
    x, ctx_1024, fside_SxS2_0, mask_BxS_bf1 = _rec_inputs()

    def _L0_xattn_setup():
        import jax, jax.numpy as jnp
        import numpy as np
        B, S, D, H = (2, 256, 128, 16)
        DH = D // H

        def _split_heads(x):
            b, s, d = x.shape
            return x.reshape(b, s, H, DH).transpose(0, 2, 1, 3)
        key = jax.random.key(seed)
        ks = jax.random.split(key, 8)
        inp = {'query': jax.random.normal(ks[0], (B, S, D), dtype=jnp.float32), 'key': jax.random.normal(ks[1], (B, S, D), dtype=jnp.float32), 'value': jax.random.normal(ks[2], (B, S, D), dtype=jnp.float32), 'attentionMask': jax.random.normal(ks[3], (S, S), dtype=jnp.float32), 'Wq': jax.random.normal(ks[4], (D, D), dtype=jnp.float32) * 0.02, 'Wk': jax.random.normal(ks[5], (D, D), dtype=jnp.float32) * 0.02, 'Wv': jax.random.normal(ks[6], (D, D), dtype=jnp.float32) * 0.02, 'Wo': jax.random.normal(ks[7], (D, D), dtype=jnp.float32) * 0.02}
        return inp
    _L0_xattn_all = _L0_xattn_setup()
    _L0_xattn_in = {k: v for k, v in _L0_xattn_all.items() if k in ('Wq', 'Wk', 'Wv', 'Wo')}
    del _L0_xattn_all

    def _L0_ffn_setup():
        import jax, jax.numpy as jnp
        import numpy as np
        import math
        EMBED_DIM = 128
        FFN_DIM = 512
        N_EXPERTS = 8
        TOP_K = 2
        CAP_FACTOR = 1.25
        key = jax.random.key(seed)
        k0, k1, k2, k3 = jax.random.split(key, 4)
        B, S = (4, 256)
        x = jax.random.normal(k0, (B, S, EMBED_DIM), dtype=jnp.float32)
        Wr = jax.random.normal(k1, (EMBED_DIM, N_EXPERTS), dtype=jnp.float32) * 0.02
        W1 = jax.random.normal(k2, (N_EXPERTS, EMBED_DIM, FFN_DIM), dtype=jnp.float32) * 0.02
        W2 = jax.random.normal(k3, (N_EXPERTS, FFN_DIM, EMBED_DIM), dtype=jnp.float32) * 0.02
        return {'x': x, 'Wr': Wr, 'W1': W1, 'W2': W2}
    _L0_ffn_all = _L0_ffn_setup()
    _L0_ffn_in = {k: v for k, v in _L0_ffn_all.items() if k in ('Wr', 'W1', 'W2')}
    del _L0_ffn_all

    def _L1_xattn_setup():
        import jax, jax.numpy as jnp
        import numpy as np
        EMBED = 128
        HEADS = 16
        HEAD_DIM = EMBED // HEADS
        EXP_DIM = 2 * HEAD_DIM

        def _feature_map(x, fm_w, fm_b):
            z = jnp.einsum('nshd,ed->nshe', x, fm_w) + fm_b
            return jnp.concatenate([jnp.exp(z), jnp.exp(-z)], axis=-1)
        key = jax.random.key(seed)
        ks = jax.random.split(key, 7)
        N, S = (4, 256)
        values = jax.random.normal(ks[0], (N, S, EMBED), dtype=jnp.float32)
        keys_ = jax.random.normal(ks[1], (N, S, EMBED), dtype=jnp.float32)
        query = jax.random.normal(ks[2], (N, S, EMBED), dtype=jnp.float32)
        fm_w = jnp.eye(HEAD_DIM, dtype=jnp.float32) + 0.02 * jax.random.normal(ks[3], (HEAD_DIM, HEAD_DIM), dtype=jnp.float32)
        fm_b = 0.02 * jax.random.normal(ks[4], (HEAD_DIM,), dtype=jnp.float32)
        fc_w = jax.random.normal(ks[5], (EMBED, HEADS * EXP_DIM), dtype=jnp.float32) * (1.0 / np.sqrt(HEADS * EXP_DIM))
        fc_b = jnp.zeros((EMBED,), dtype=jnp.float32)
        return {'values': values, 'keys': keys_, 'query': query, 'fm_w': fm_w, 'fm_b': fm_b, 'fc_w': fc_w, 'fc_b': fc_b}
    _L1_xattn_all = _L1_xattn_setup()
    _L1_xattn_in = {k: v for k, v in _L1_xattn_all.items() if k in ('fm_w', 'fm_b', 'fc_w', 'fc_b')}
    del _L1_xattn_all

    def _L1_ffn_setup():
        import jax, jax.numpy as jnp
        import numpy as np
        E = 16
        F_C = 2.0
        D = 128
        I = 4 * D
        IS = 2 * D
        B, S = (4, 128)
        key = jax.random.key(seed)
        ks = jax.random.split(key, 8)
        w = 0.02
        return {'hidden_states': jax.random.normal(ks[0], (B, S, D), dtype=jnp.float32), 'gate_w': jax.random.normal(ks[1], (E, D), dtype=jnp.float32) * w, 'Wg': jax.random.normal(ks[2], (E, I, D), dtype=jnp.float32) * w, 'Wu': jax.random.normal(ks[3], (E, I, D), dtype=jnp.float32) * w, 'Wd': jax.random.normal(ks[4], (E, D, I), dtype=jnp.float32) * w, 'Sg': jax.random.normal(ks[5], (IS, D), dtype=jnp.float32) * w, 'Su': jax.random.normal(ks[6], (IS, D), dtype=jnp.float32) * w, 'Sd': jax.random.normal(ks[7], (D, IS), dtype=jnp.float32) * w}
    _L1_ffn_all = _L1_ffn_setup()
    _L1_ffn_in = {k: v for k, v in _L1_ffn_all.items() if k in ('gate_w', 'Wg', 'Wu', 'Wd', 'Sg', 'Su', 'Sd')}
    del _L1_ffn_all

    def _L2_xattn_setup():
        import jax, jax.numpy as jnp
        import numpy as np
        NUM_HEADS = 16
        TOKEN_DIM = 128
        D_HEAD = TOKEN_DIM // NUM_HEADS

        def masked_softmax(scores, mask):
            scores = jnp.clip(scores, -50.0, 50.0)
            exp_scores = jnp.exp(scores)
            if mask is not None:
                exp_scores = jnp.where(mask, exp_scores, 0.0)
            denom = jnp.sum(exp_scores, axis=-1, keepdims=True)
            denom = jnp.where(denom <= 0.0, 1.0, denom)
            return exp_scores / denom
        key = jax.random.key(seed)
        ks = jax.random.split(key, 8)
        B, Sq, Sk = (2, 256, 256)
        scale = 1.0 / np.sqrt(TOKEN_DIM)
        return {'Q': jax.random.normal(ks[0], (B, Sq, TOKEN_DIM), dtype=jnp.float32), 'K': jax.random.normal(ks[1], (B, Sk, TOKEN_DIM), dtype=jnp.float32), 'V': jax.random.normal(ks[2], (B, Sk, TOKEN_DIM), dtype=jnp.float32), 'mask': jnp.ones((B, Sq), dtype=bool), 'W_q': jax.random.normal(ks[3], (TOKEN_DIM, TOKEN_DIM), dtype=jnp.float32) * scale, 'W_k': jax.random.normal(ks[4], (TOKEN_DIM, TOKEN_DIM), dtype=jnp.float32) * scale, 'W_v': jax.random.normal(ks[5], (TOKEN_DIM, TOKEN_DIM), dtype=jnp.float32) * scale, 'W_o': jax.random.normal(ks[6], (TOKEN_DIM, TOKEN_DIM), dtype=jnp.float32) * scale}
    _L2_xattn_all = _L2_xattn_setup()
    _L2_xattn_in = {k: v for k, v in _L2_xattn_all.items() if k in ('W_q', 'W_k', 'W_v', 'W_o')}
    del _L2_xattn_all

    def _L2_ffn_setup():
        import jax, jax.numpy as jnp
        import numpy as np
        B, S, D = (2, 256, 128)
        E, K, F = (16, 2, 64)
        FS = 128
        key = jax.random.key(seed)
        ks = jax.random.split(key, 8)

        def w(k, shape, fan_in):
            return jax.random.normal(k, shape, jnp.float32) / np.sqrt(fan_in).astype(np.float32)
        return {'x': jax.random.normal(ks[0], (B, S, D), jnp.float32), 'Wr': w(ks[1], (D, E), D), 'Wg': w(ks[2], (E, D, F), D), 'Wu': w(ks[3], (E, D, F), D), 'Wd': w(ks[4], (E, F, D), F), 'Sg': w(ks[5], (D, FS), D), 'Su': w(ks[6], (D, FS), D), 'Sd': w(ks[7], (FS, D), FS)}
    _L2_ffn_all = _L2_ffn_setup()
    _L2_ffn_in = {k: v for k, v in _L2_ffn_all.items() if k in ('Wr', 'Wg', 'Wu', 'Wd', 'Sg', 'Su', 'Sd')}
    del _L2_ffn_all

    def _L3_xattn_setup():
        import jax, jax.numpy as jnp
        import numpy as np
        KDIM = 64
        key = jax.random.key(seed)
        ks = jax.random.split(key, 7)
        B, S, M, H, D = (4, 256, 128, 16, 64)
        q = jax.random.normal(ks[0], (B, S, M), dtype=jnp.float32)
        k = jax.random.normal(ks[1], (B, S, M), dtype=jnp.float32)
        v = jax.random.normal(ks[2], (B, S, M), dtype=jnp.float32)
        sc = 1.0 / np.sqrt(M)
        Wq = jax.random.normal(ks[3], (H, M, D), dtype=jnp.float32) * sc
        Wk = jax.random.normal(ks[4], (H, M, D), dtype=jnp.float32) * sc
        Wv = jax.random.normal(ks[5], (H, M, D), dtype=jnp.float32) * sc
        Wo = jax.random.normal(ks[6], (H * D, M), dtype=jnp.float32) * (1.0 / np.sqrt(H * D))
        return {'q': q, 'k': k, 'v': v, 'Wq': Wq, 'Wk': Wk, 'Wv': Wv, 'Wo': Wo}
    _L3_xattn_all = _L3_xattn_setup()
    _L3_xattn_in = {k: v for k, v in _L3_xattn_all.items() if k in ('Wq', 'Wk', 'Wv', 'Wo')}
    del _L3_xattn_all

    def _L3_ffn_setup():
        import jax, jax.numpy as jnp
        import numpy as np
        S, B, H, I, E = (64, 2, 128, 352, 8)
        key = jax.random.key(seed)
        ks = jax.random.split(key, 5)
        return {'hidden_states': jax.random.normal(ks[0], (S, B, H), dtype=jnp.float32), 'router_w': jax.random.normal(ks[1], (E, H), dtype=jnp.float32) * 0.02, 'gate_w': jax.random.normal(ks[2], (E, I, H), dtype=jnp.float32) * 0.02, 'up_w': jax.random.normal(ks[3], (E, I, H), dtype=jnp.float32) * 0.02, 'down_w': jax.random.normal(ks[4], (E, H, I), dtype=jnp.float32) * 0.02}
    _L3_ffn_all = _L3_ffn_setup()
    _L3_ffn_in = {k: v for k, v in _L3_ffn_all.items() if k in ('router_w', 'gate_w', 'up_w', 'down_w')}
    del _L3_ffn_all
    return {'x': x, 'ctx_1024': ctx_1024, 'fside_SxS2_0': fside_SxS2_0, 'mask_BxS_bf1': mask_BxS_bf1, 'L0_xattn_Wq': _L0_xattn_in['Wq'], 'L0_xattn_Wk': _L0_xattn_in['Wk'], 'L0_xattn_Wv': _L0_xattn_in['Wv'], 'L0_xattn_Wo': _L0_xattn_in['Wo'], 'L0_ffn_Wr': _L0_ffn_in['Wr'], 'L0_ffn_W1': _L0_ffn_in['W1'], 'L0_ffn_W2': _L0_ffn_in['W2'], 'L1_xattn_fm_w': _L1_xattn_in['fm_w'], 'L1_xattn_fm_b': _L1_xattn_in['fm_b'], 'L1_xattn_fc_w': _L1_xattn_in['fc_w'], 'L1_xattn_fc_b': _L1_xattn_in['fc_b'], 'L1_ffn_gate_w': _L1_ffn_in['gate_w'], 'L1_ffn_Wg': _L1_ffn_in['Wg'], 'L1_ffn_Wu': _L1_ffn_in['Wu'], 'L1_ffn_Wd': _L1_ffn_in['Wd'], 'L1_ffn_Sg': _L1_ffn_in['Sg'], 'L1_ffn_Su': _L1_ffn_in['Su'], 'L1_ffn_Sd': _L1_ffn_in['Sd'], 'L2_xattn_W_q': _L2_xattn_in['W_q'], 'L2_xattn_W_k': _L2_xattn_in['W_k'], 'L2_xattn_W_v': _L2_xattn_in['W_v'], 'L2_xattn_W_o': _L2_xattn_in['W_o'], 'L2_ffn_Wr': _L2_ffn_in['Wr'], 'L2_ffn_Wg': _L2_ffn_in['Wg'], 'L2_ffn_Wu': _L2_ffn_in['Wu'], 'L2_ffn_Wd': _L2_ffn_in['Wd'], 'L2_ffn_Sg': _L2_ffn_in['Sg'], 'L2_ffn_Su': _L2_ffn_in['Su'], 'L2_ffn_Sd': _L2_ffn_in['Sd'], 'L3_xattn_Wq': _L3_xattn_in['Wq'], 'L3_xattn_Wk': _L3_xattn_in['Wk'], 'L3_xattn_Wv': _L3_xattn_in['Wv'], 'L3_xattn_Wo': _L3_xattn_in['Wo'], 'L3_ffn_router_w': _L3_ffn_in['router_w'], 'L3_ffn_gate_w': _L3_ffn_in['gate_w'], 'L3_ffn_up_w': _L3_ffn_in['up_w'], 'L3_ffn_down_w': _L3_ffn_in['down_w']}

def reference(x, ctx_1024, fside_SxS2_0, mask_BxS_bf1, L0_xattn_Wq, L0_xattn_Wk, L0_xattn_Wv, L0_xattn_Wo, L0_ffn_Wr, L0_ffn_W1, L0_ffn_W2, L1_xattn_fm_w, L1_xattn_fm_b, L1_xattn_fc_w, L1_xattn_fc_b, L1_ffn_gate_w, L1_ffn_Wg, L1_ffn_Wu, L1_ffn_Wd, L1_ffn_Sg, L1_ffn_Su, L1_ffn_Sd, L2_xattn_W_q, L2_xattn_W_k, L2_xattn_W_v, L2_xattn_W_o, L2_ffn_Wr, L2_ffn_Wg, L2_ffn_Wu, L2_ffn_Wd, L2_ffn_Sg, L2_ffn_Su, L2_ffn_Sd, L3_xattn_Wq, L3_xattn_Wk, L3_xattn_Wv, L3_xattn_Wo, L3_ffn_router_w, L3_ffn_gate_w, L3_ffn_up_w, L3_ffn_down_w):
    import jax
    import jax.numpy as jnp

    def _L0_xattn_ref(query, key, value, attentionMask, Wq, Wk, Wv, Wo):
        import jax, jax.numpy as jnp
        import numpy as np
        B, S, D, H = (2, 256, 128, 16)
        DH = D // H

        def _split_heads(x):
            b, s, d = x.shape
            return x.reshape(b, s, H, DH).transpose(0, 2, 1, 3)
        q = _split_heads(query @ Wq.T)
        k = _split_heads(key @ Wk.T)
        v = _split_heads(value @ Wv.T)
        scale = 1.0 / jnp.sqrt(jnp.float32(DH))
        logits = jnp.einsum('bhqd,bhkd->bhqk', q, k) * scale
        logits = logits + attentionMask[None, None, :, :]
        attn = jax.nn.softmax(logits, axis=-1)
        out = jnp.einsum('bhqk,bhkd->bhqd', attn, v)
        out = out.transpose(0, 2, 1, 3).reshape(query.shape[0], query.shape[1], D)
        return out @ Wo.T

    def _L0_ffn_ref(x, Wr, W1, W2):
        import jax, jax.numpy as jnp
        import numpy as np
        import math
        EMBED_DIM = 128
        FFN_DIM = 512
        N_EXPERTS = 8
        TOP_K = 2
        CAP_FACTOR = 1.25
        B, S, D = x.shape
        t = B * S
        xf = x.reshape(t, D)
        probs = jax.nn.softmax(xf.astype(jnp.float32) @ Wr, axis=-1)
        topk_probs, topk_experts = jax.lax.top_k(probs, TOP_K)
        cap = max(math.ceil(t * TOP_K * CAP_FACTOR / N_EXPERTS), 1)
        y = jnp.zeros_like(xf)
        for e in range(N_EXPERTS):
            mask = topk_experts == e
            gate = jnp.sum(jnp.where(mask, topk_probs, 0.0), axis=-1)
            has = jnp.any(mask, axis=-1)
            g_masked = jnp.where(has, gate, -jnp.inf)
            vals, idx = jax.lax.top_k(g_masked, cap)
            g = jnp.where(jnp.isfinite(vals), vals, 0.0)
            xe = xf[idx]
            h = jax.nn.relu(xe @ W1[e]) @ W2[e]
            y = y.at[idx].add(g[:, None] * h)
        return y.reshape(B, S, D)

    def _L1_xattn_ref(values, keys, query, fm_w, fm_b, fc_w, fc_b):
        import jax, jax.numpy as jnp
        import numpy as np
        EMBED = 128
        HEADS = 16
        HEAD_DIM = EMBED // HEADS
        EXP_DIM = 2 * HEAD_DIM

        def _feature_map(x, fm_w, fm_b):
            z = jnp.einsum('nshd,ed->nshe', x, fm_w) + fm_b
            return jnp.concatenate([jnp.exp(z), jnp.exp(-z)], axis=-1)
        N, S, _ = query.shape
        v = values.reshape(N, -1, HEADS, HEAD_DIM)
        k = keys.reshape(N, -1, HEADS, HEAD_DIM)
        q = query.reshape(N, -1, HEADS, HEAD_DIM)
        v, k, q = (_feature_map(x, fm_w, fm_b) for x in (v, k, q))
        scores = jnp.einsum('nqhd,nkhd->nhqk', q, k) / jnp.sqrt(jnp.float32(EMBED))
        attn = jax.nn.softmax(scores, axis=-1)
        out = jnp.einsum('nhql,nlhd->nqhd', attn, v)
        out = out.reshape(N, S, HEADS * EXP_DIM)
        return out @ fc_w.T + fc_b

    def _L1_ffn_ref(hidden_states, gate_w, Wg, Wu, Wd, Sg, Su, Sd):
        import jax, jax.numpy as jnp
        import numpy as np
        E = 16
        F_C = 2.0
        D = 128
        I = 4 * D
        IS = 2 * D
        B, S = (4, 128)
        b, s, d = hidden_states.shape
        T = b * s
        C = int(T * F_C / E)
        flat_x = hidden_states.reshape(T, d)
        logits = flat_x @ gate_w.T
        scores = jax.nn.softmax(logits, axis=-1).T
        topk_weight, topk_idx = jax.lax.top_k(scores, C)
        xg = flat_x[topk_idx]
        g = jnp.einsum('ecd,eid->eci', xg, Wg)
        u = jnp.einsum('ecd,eid->eci', xg, Wu)
        h = jax.nn.gelu(g, approximate=False) * u
        eo = jnp.einsum('eci,edi->ecd', h, Wd)
        eo = eo * topk_weight[..., None]
        flat_out = jnp.zeros_like(flat_x).at[topk_idx.reshape(-1)].add(eo.reshape(-1, d))
        out = flat_out.reshape(b, s, d)
        sg = hidden_states @ Sg.T
        su = hidden_states @ Su.T
        shared = jax.nn.gelu(sg, approximate=False) * su @ Sd.T
        return out + shared

    def _L2_xattn_ref(Q, K, V, mask, W_q, W_k, W_v, W_o):
        import jax, jax.numpy as jnp
        import numpy as np
        NUM_HEADS = 16
        TOKEN_DIM = 128
        D_HEAD = TOKEN_DIM // NUM_HEADS

        def masked_softmax(scores, mask):
            scores = jnp.clip(scores, -50.0, 50.0)
            exp_scores = jnp.exp(scores)
            if mask is not None:
                exp_scores = jnp.where(mask, exp_scores, 0.0)
            denom = jnp.sum(exp_scores, axis=-1, keepdims=True)
            denom = jnp.where(denom <= 0.0, 1.0, denom)
            return exp_scores / denom
        B = Q.shape[0]
        q = (Q @ W_q.T).reshape(B, -1, NUM_HEADS, D_HEAD).transpose(0, 2, 1, 3)
        k = (K @ W_k.T).reshape(B, -1, NUM_HEADS, D_HEAD).transpose(0, 2, 1, 3)
        v = (V @ W_v.T).reshape(B, -1, NUM_HEADS, D_HEAD).transpose(0, 2, 1, 3)
        scores = jnp.einsum('bhqd,bhkd->bhqk', q, k) / np.sqrt(D_HEAD)
        m = mask[:, None, :, None] if mask is not None else None
        attn = masked_softmax(scores, m)
        out = jnp.einsum('bhqk,bhkd->bhqd', attn, v)
        out = out.transpose(0, 2, 1, 3).reshape(B, -1, NUM_HEADS * D_HEAD)
        return out @ W_o.T

    def _L2_ffn_ref(x, Wr, Wg, Wu, Wd, Sg, Su, Sd):
        import jax, jax.numpy as jnp
        import numpy as np
        B, S, D = (2, 256, 128)
        E, K, F = (16, 2, 64)
        FS = 128
        b, s, d = x.shape
        T = b * s
        xf = x.reshape(T, d)
        shared = jax.nn.silu(xf @ Sg) * (xf @ Su) @ Sd
        probs = jax.nn.softmax(xf @ Wr, axis=-1)
        topk_p, topk_i = jax.lax.top_k(probs, K)
        n_exp = Wr.shape[1]
        cw = jnp.zeros((T, n_exp), x.dtype).at[jnp.arange(T)[:, None], topk_i].add(topk_p)

        def step(acc, ew):
            wg, wu, wd, c = ew
            y = jax.nn.silu(xf @ wg) * (xf @ wu) @ wd
            return (acc + y * c[:, None], None)
        routed, _ = jax.lax.scan(step, jnp.zeros_like(xf), (Wg, Wu, Wd, cw.T))
        return (routed + shared).reshape(b, s, d)

    def _L3_xattn_ref(q, k, v, Wq, Wk, Wv, Wo):
        import jax, jax.numpy as jnp
        import numpy as np
        KDIM = 64
        Q = jnp.einsum('bsm,hmd->bhsd', q, Wq)
        K = jnp.einsum('bsm,hmd->bhsd', k, Wk)
        V = jnp.einsum('bsm,hmd->bhsd', v, Wv)
        scores = jnp.einsum('bhsd,bhtd->bhst', Q, K) / jnp.sqrt(jnp.asarray(KDIM, Q.dtype))
        A = jax.nn.softmax(scores, axis=-1)
        O = jnp.einsum('bhst,bhtd->bhsd', A, V)
        B, H, S, D = O.shape
        Ocat = jnp.transpose(O, (0, 2, 1, 3)).reshape(B, S, H * D)
        return Ocat @ Wo

    def _L3_ffn_ref(hidden_states, router_w, gate_w, up_w, down_w):
        import jax, jax.numpy as jnp
        import numpy as np
        S, B, H, I, E = (64, 2, 128, 352, 8)
        router_logits = jnp.einsum('sbh,eh->sbe', hidden_states, router_w)
        routing_indices = jnp.argmax(router_logits, axis=-1)
        out = jnp.zeros_like(hidden_states)
        for e in range(E):
            mask = (routing_indices == e)[..., None]
            xe = jnp.where(mask, hidden_states, 0.0)
            g = jnp.einsum('sbh,ih->sbi', xe, gate_w[e])
            u = jnp.einsum('sbh,ih->sbi', xe, up_w[e])
            ye = jnp.einsum('sbi,hi->sbh', jax.nn.silu(g) * u, down_w[e])
            out = out + jnp.where(mask, ye, 0.0)
        return out
    x = x + _L0_xattn_ref(_layernorm(x, axis=-1), ctx_1024, ctx_1024, fside_SxS2_0, L0_xattn_Wq, L0_xattn_Wk, L0_xattn_Wv, L0_xattn_Wo)
    x = x + _L0_ffn_ref(_layernorm(x, axis=-1), L0_ffn_Wr, L0_ffn_W1, L0_ffn_W2)
    x = x + _L1_xattn_ref(ctx_1024, ctx_1024, _layernorm(x, axis=-1), L1_xattn_fm_w, L1_xattn_fm_b, L1_xattn_fc_w, L1_xattn_fc_b)
    x = x + _L1_ffn_ref(_layernorm(x, axis=-1), L1_ffn_gate_w, L1_ffn_Wg, L1_ffn_Wu, L1_ffn_Wd, L1_ffn_Sg, L1_ffn_Su, L1_ffn_Sd)
    x = x + _L2_xattn_ref(_layernorm(x, axis=-1), ctx_1024, ctx_1024, mask_BxS_bf1, L2_xattn_W_q, L2_xattn_W_k, L2_xattn_W_v, L2_xattn_W_o)
    x = x + _L2_ffn_ref(_layernorm(x, axis=-1), L2_ffn_Wr, L2_ffn_Wg, L2_ffn_Wu, L2_ffn_Wd, L2_ffn_Sg, L2_ffn_Su, L2_ffn_Sd)
    x = x + _L3_xattn_ref(_layernorm(x, axis=-1), ctx_1024, ctx_1024, L3_xattn_Wq, L3_xattn_Wk, L3_xattn_Wv, L3_xattn_Wo)
    x = x + _L3_ffn_ref(_layernorm(x, axis=-1), L3_ffn_router_w, L3_ffn_gate_w, L3_ffn_up_w, L3_ffn_down_w)
    return x

_drawn_inputs = setup_inputs


def setup_inputs(seed=0):
    import zlib

    import numpy as np

    out = dict(_drawn_inputs(seed))
    spreads = {'L1_xattn_fc_b': (0.0, 0.8)}
    factors = {'fside_SxS2_0': 8.0,
     'L0_xattn_Wq': 8.0,
     'L0_xattn_Wk': 8.0,
     'L0_ffn_Wr': 3.536,
     'L0_ffn_W1': 4.474,
     'L0_ffn_W2': 3.754,
     'L1_ffn_gate_w': 8.0,
     'L1_ffn_Wg': 8.0,
     'L1_ffn_Wu': 8.0,
     'L1_ffn_Wd': 8.0,
     'L1_ffn_Sg': 8.0,
     'L1_ffn_Su': 8.0,
     'L1_ffn_Sd': 8.0,
     'L2_xattn_W_q': 2.828,
     'L2_xattn_W_k': 3.223,
     'L2_ffn_Wr': 3.786,
     'L2_ffn_Wg': 3.897,
     'L2_ffn_Wu': 3.285,
     'L2_ffn_Wd': 3.412,
     'L3_xattn_Wq': 3.133,
     'L3_xattn_Wk': 2.871,
     'L3_ffn_router_w': 8.0,
     'L3_ffn_gate_w': 8.0,
     'L3_ffn_up_w': 8.0,
     'L3_ffn_down_w': 8.0}
    for name, (base, spread) in spreads.items():
        noise = np.random.default_rng([zlib.crc32(name.encode()), seed]).standard_normal(out[name].shape)
        drawn = base * np.exp(spread * noise) if base else spread * noise
        out[name] = jnp.asarray(drawn.astype(out[name].dtype))
    for name, factor in factors.items():
        out[name] = (out[name] * factor).astype(out[name].dtype)
    return out
```

```python
from contextlib import ExitStack

import concourse.bass as bass
from concourse import mybir

ALU = mybir.AluOpType
ACT = mybir.ActivationFunctionType
AX = mybir.AxisListType
F32 = mybir.dt.float32
BF16 = mybir.dt.bfloat16
I32 = mybir.dt.int32
U8 = mybir.dt.uint8

P = 128
D = 128
TOK = 1024
T = TOK // P
B = 4
KEYS = 64
BK = B * KEYS
H = 16
PAIRS = H // 2
HALF = TOK // 2
EPS = 1e-5
ND = [8, 16, 8, 64]
SCALE = [8 ** -0.5, 128 ** -0.5, 8 ** -0.5, 64 ** -0.5]
CLIP = 50.0
E = [8, 16, 16, 8]
CAP = [320, 128]
CREDIT = 2
N_SUB = 8

W_COLS = [512 + 512, 3 * 512, 3 * 128, 352 + 352 + 3 * 128]
F3_M = [128, 128, 96]
WMAX = 3 * 512


def build(nc, x_in, ctxT, fside, qmask, aw0, aw1, fmT, fmb, fcb, aw2, aw3,
          wr0, wr1, wr2, wr3, fw0, fw1, fw2, fw3, sh1, sh2, out):
    with ExitStack() as ctx:
        def sb(name, shape, dt=F32):
            return ctx.enter_context(nc.sbuf_tensor(name, shape, dt))

        sems = {}

        def S(name):
            if name not in sems:
                sems[name] = ctx.enter_context(nc.semaphore(name.replace(" ", "_")))
            return sems[name]

        bank = [ctx.enter_context(nc.psum_tensor(f"bank{i}", [P, 512], F32)) for i in range(8)]

        x = sb("x", [P, T, D])
        xn = sb("xn", [P, T, D])
        xnT = sb("xnT", [P, TOK])
        st6 = sb("st6", [P, T, 6])
        mv = sb("mv", [P, T, 2])
        ve = sb("ve", [P, T])
        rstd = sb("rstd", [P, T])
        neghalf = sb("neghalf", [P, T])
        ident = sb("ident", [P, P])
        hm8 = sb("hm8", [P, 16])
        hm16 = sb("hm16", [P, 8])
        hm64 = sb("hm64", [P, 2])
        same8 = sb("same8", [P, P])
        same16 = sb("same16", [P, P])
        before8 = sb("before8", [P, P])
        before16 = sb("before16", [P, P])
        iota_row = sb("iota_row", [P, P])
        iota_col = sb("iota_col", [P, 1])
        chan_i = sb("chan_i", [P, 1], I32)
        sgn_i = sb("sgn_i", [P, 1], I32)
        sgn = sb("sgn", [P, 1])
        mod_a = sb("mod_a", [P, 2], I32)
        mod_r = sb("mod_r", [P, 2, P], I32)
        mod_f = sb("mod_f", [P, 2])
        mod_rf = sb("mod_rf", [P, 2, P])
        rev = sb("rev", [P, 16])
        zero_bf = sb("zero_bf", [P, 512], BF16)
        ones_row = sb("ones_row", [1, P])
        ctx_sb = sb("ctx_sb", [P, BK])
        ctx_dup = sb("ctx_dup", [P, B, 2, KEYS])
        fside_sb = sb("fside_sb", [P, 2, KEYS])
        qm8 = sb("qm8", [P, T], U8)
        qm = sb("qm", [P, T])
        aw0_sb = sb("aw0_sb", [P, 4, D])
        aw1_sb = sb("aw1_sb", [P, 2, D])
        aw2_sb = sb("aw2_sb", [P, 4, D])
        aw3_sb = sb("aw3_sb", [P, 4, 8, D])
        fmrep = sb("fmrep", [P, 9])
        fm2 = sb("fm2", [P, 2, 8, 2, 8])
        fmb_all = sb("fmb_all", [P, 8])
        bias_col = sb("bias_col", [P, 1])
        fcb_row = sb("fcb_row", [1, D])
        A = sb("A", [P, B, H, KEYS])
        Vb = sb("Vb", [P, B * PAIRS * 128])
        projT = sb("projT", [P, 2, BK])
        kblk = sb("kblk", [P, 2, TOK])
        xa = sb("xa", [P, 2, D])
        xaT = sb("xaT", [P, 2, P])
        qf = sb("qf", [P, 2, 2, P])
        lg = sb("lg", [P, 2, H, KEYS])
        pr = sb("pr", [P, 2, H, KEYS])
        mx = sb("mx", [P, 2, H])
        rden = sb("rden", [P, 2, H])
        rden2 = sb("rden2", [P, 2, H])
        PT = sb("PT", [P, 2, 2, 512])
        on = sb("on", [P, 2, 256])
        onT = sb("onT", [P, 2, 256])
        wr_sb = [sb(f"wr{i}_sb", [P, E[i]]) for i in range(4)]
        rl = sb("rl", [P, T * 16])
        rp = sb("rp", [P, T * 16])
        rq = sb("rq", [P, T * 16])
        rk = sb("rk", [P, T * 16])
        r1 = sb("r1", [P, T * 16])
        r2 = sb("r2", [P, T * 16])
        rm = sb("rm", [P, T])
        rr = sb("rr", [P, T])
        gts = sb("gts", [P, P])
        cur = sb("cur", [P, 1], I32)
        stp = sb("stp", [P, 3], I32)
        cand = sb("cand", [P, 3], I32)
        junk = sb("junk", [P, P])
        cnt = sb("cnt", [P, 3])
        nsat = sb("nsat", [P, 1])
        junk3 = sb("junk3", [P, 3])
        addb = sb("addb", [P, 1], I32)
        tgt = sb("tgt", [P, P])
        teq = sb("teq", [P, P])
        tcum = sb("tcum", [P, P])
        tsel = sb("tsel", [P, P])
        zrow = sb("zrow", [P, P])
        tn = sb("tn", [P, 2])
        tcol = sb("tcol", [P, 4])
        gfin = sb("gfin", [P, P])
        slotc = sb("slotc", [P, P])
        wring = sb("wring", [P, 4, WMAX])
        gb = sb("gb", [P, 2, TOK])
        xg = PTs = lg[:, :, :, :].rearrange("p j h k -> p j (h k)")
        sg = sb("sg", [P, 2, 512])
        hh = PT[:, :, :, :].rearrange("p a b n -> p (a b) n")
        yT = sb("yT", [P, 2, 512])
        sh1_sb = sb("sh1_sb", [P, 6, P])
        sh2_sb = sb("sh2_sb", [P, 3, P])
        xs = sb("xs", [P, 3, T, D], BF16)
        xres = sb("xres", [P, T, D])
        ps = sb("ps", [P, T, 16, 3], BF16)
        pres = sb("pres", [P, T, 16])
        P4 = [v.bitcast(BF16).rearrange("p (t e c) -> p t e c", t=T, e=4)
              for v in (pr[:, :, :, :].rearrange("p j h k -> p (j h k)"), kblk[:, :, :].rearrange("p j n -> p (j n)"))]
        xgT = sb("xgT", [P, 4, P])
        wcol = sb("wcol", [P, 2])
        eo = sb("eo", [P, 2, P])

        gdram = [nc.dram_tensor(f"gates{i}", (T, E[i], P), F32, kind="Internal").ap() for i in range(4)]

        block = ctx.enter_context(nc.Block())
        NP = [T * e for e in E]

        def same(layer):
            return (same8 if E[layer] == 8 else same16)[0:NP[layer], 0:NP[layer]]

        def before(layer):
            return (before8 if E[layer] == 8 else before16)[0:NP[layer], 0:NP[layer]]

        def hmask(layer):
            return {8: hm8, 16: hm16, 64: hm64}[ND[layer]]

        def vview(layer):
            n = ND[layer] + 1
            return Vb[:, 0:B * PAIRS * 2 * n].rearrange("p (b c s n) -> p b c s n", b=B, c=PAIRS, s=2)

        VP3 = Vb[:, :].rearrange("p (b c n) -> p b c n", b=B, c=PAIRS)

        def unit_view(layer, slot):
            return wring[:, slot, 0:W_COLS[layer]]

        LOADS = [[0, 0, 0, 0], [4, 4, 0, 0], [8, 8, 4, 4], [12, 12, 4, 4]]
        SLOTS = [2, 4, 2, 2]
        UNITS = [8, 16, 8, 8]

        def done_value(layer, u):
            return {0: 8 * u + 12, 1: u + 7, 2: 2 * u + 6, 3: 6 * u + 8}[layer]

        UPS = {0: 8, 3: 6}

        def route_layers():
            return [i for i in range(4) if 2 * i + 1 < N_SUB]

        attn_layers = [i for i in range(4) if 2 * i < N_SUB]
        last_ln = N_SUB

        @block.sync
        def _(sp):
            sp.dma_start(x[:, :, :], x_in.rearrange("(t p) d -> p t d", p=P)).then_inc(S("x_in"), 16)
            sp.dma_start(ctx_sb[:, :], ctxT).then_inc(S("ctx_in"), 16)
            for c in range(2):
                sp.dma_start(ctx_dup[:, :, c, :], ctxT.rearrange("p (b k) -> p b k", b=B)).then_inc(S("ctx_in"), 16)
            sp.dma_start(aw0_sb[:, :, :], aw0).then_inc(S("aw0_in"), 16)
            sp.dma_start(fside_sb[:, :, :], fside.rearrange("(j p) k -> p j k", p=P)).then_inc(S("aw0_in"), 16)
            for i, w in enumerate((wr0, wr1, wr2, wr3)):
                sp.dma_start(wr_sb[i][:, :], w).then_inc(S("wr_in"), 16)
            sp.dma_start(aw1_sb[:, :, :], aw1).then_inc(S("aw1_in"), 16)
            sp.dma_start(fmrep[:, :], fmT).then_inc(S("aw1_in"), 16)
            sp.dma_start(fmb_all[:, :], fmb.rearrange("(a e) -> a e", a=1).broadcast_to([P, 8])).then_inc(S("aw1_in"), 16)
            sp.dma_start(fcb_row[:, :], fcb.rearrange("(a e) -> a e", a=1)).then_inc(S("aw1_in"), 16)
            sp.dma_start(qm8[:, :], qmask).then_inc(S("aw2_in"), 16)
            sp.dma_start(aw2_sb[:, :, :], aw2).then_inc(S("aw2_in"), 16)
            sp.dma_start(sh1_sb[:, :, :], sh1).then_inc(S("sh_in"), 16)
            sp.dma_start(sh2_sb[:, :, :], sh2).then_inc(S("sh_in"), 16)
            sp.dma_start(aw3_sb[:, :, :, :], aw3).then_inc(S("aw3_in"), 16)

            fw = [fw0, fw1, fw2, fw3]

            def load_weights(layer, u, slot):
                sp.dma_start(unit_view(layer, slot), fw[layer][u]).then_inc(S(f"w_in{slot}"), 16)

            def load_gates(layer, u, slot):
                if layer == 2:
                    for c in range(2):
                        sp.dma_start(gb[64 * c:64 * c + 64, slot, :].rearrange("p (t n) -> p t n", t=T),
                                     gdram[2][:, 2 * u + c, :].unsqueeze(0).broadcast_to([64, T, P])
                                     ).then_inc(S(f"gb_in{slot}"), 16)
                else:
                    sp.dma_start(gb[:, slot, :].rearrange("p (t n) -> p t n", t=T),
                                 gdram[layer][:, u, :].unsqueeze(0).broadcast_to([P, T, P])
                                 ).then_inc(S(f"gb_in{slot}"), 16)

            for layer in route_layers():
                n = SLOTS[layer]
                if layer:
                    sp.wait_ge(S(f"down{layer - 1}"), done_value(layer - 1, UNITS[layer - 1] - 1))
                for u in range(n):
                    load_weights(layer, u, u)
                sp.wait_ge(S("gates_final"), layer + 1)
                sp.dma_start(gdram[layer].rearrange("t e p -> (t e) p"), gfin[0:NP[layer], :]).then_inc(S("gates_out"), 16)
                sp.wait_ge(S("gates_out"), 16 * (layer + 1))
                for u in range(2):
                    load_gates(layer, u, u)

                def refill(u, slot, gslot):
                    if slot is not None:
                        sp.wait_ge(S(f"down{layer}"), done_value(layer, u - n))
                        load_weights(layer, u, slot)
                    if layer == 2:
                        sp.wait_ge(S("h2"), 2 * u + 2)
                    else:
                        sp.wait_ge(S(f"gates_used{layer}"), u + CREDIT - 1)
                    load_gates(layer, u, gslot)

                if layer == 1:
                    refill(2, None, 0)
                    refill(3, None, 1)
                with sp.Fori(1, UNITS[layer] // n) as i:
                    for s in range(n):
                        refill(i * n + s, s, s % 2)
            sp.wait_ge(S("final"), 1)
            sp.dma_start(out.rearrange("(t p) d -> p t d", p=P), x[:, :, :]).then_inc(S("out_done"), 16)
            sp.wait_ge(S("out_done"), 16)

        @block.gpsimd
        def _(pool):
            step = [0]

            def chain(ins):
                ins.then_inc(S("pool_step"), 1)
                step[0] += 1
                pool.wait_ge(S("pool_step"), step[0])

            chain(pool.memset(neghalf[:, :], -0.5))
            chain(pool.memset(ones_row[:, :], 1.0))
            chain(pool.memset(zero_bf[:, :], 0.0))
            chain(pool.memset(zrow[:, :], 0.0))
            chain(pool.memset(ident[:, :], 0.0))
            chain(pool.affine_select(out=ident[:, :], in_=ident[:, :], compare_op=ALU.not_equal, fill=1.0,
                                     base=0, pattern=[[-1, P]], channel_multiplier=1))
            for m, nd in ((hm8, 8), (hm16, 16), (hm64, 64)):
                nh = P // nd
                chain(pool.memset(m[:, :], 1.0))
                chain(pool.affine_select(out=m[:, :], in_=m[:, :], compare_op=ALU.is_ge, fill=0.0,
                                         base=0, pattern=[[-nd, nh]], channel_multiplier=1))
                chain(pool.affine_select(out=m[:, :], in_=m[:, :], compare_op=ALU.is_ge, fill=0.0,
                                         base=nd - 1, pattern=[[nd, nh]], channel_multiplier=-1))
            chain(pool.iota(iota_row[:, :], pattern=[[1, P]], base=0, channel_multiplier=0,
                      allow_small_or_imprecise_dtypes=True))
            chain(pool.iota(iota_col[:, :], pattern=[[1, 1]], base=0, channel_multiplier=1,
                      allow_small_or_imprecise_dtypes=True))
            chain(pool.iota(rev[:, :], pattern=[[-1, 16]], base=16, channel_multiplier=0,
                      allow_small_or_imprecise_dtypes=True))
            chain(pool.iota(chan_i[:, :], pattern=[[1, 1]], base=0, channel_multiplier=1))
            chain(pool.iota(mod_r[:, 0, :], pattern=[[1, P]], base=0, channel_multiplier=0))
            pool.memset(Vb[:, :], 0.0).then_inc(S("const"), 1)
            pool.wait_ge(S("const"), 1)

            def blocks(layer):
                m = hmask(layer)
                if ND[layer] == 8:
                    for b in range(B):
                        pool.wait_ge(S(f"projT{layer}"), 1)
                        if b >= 2:
                            pool.wait_ge(S(f"kmm{layer}"), 2 * (b - 1))
                        elif layer:
                            pool.wait_ge(S("attn_done"), layer)
                        pool.tensor_tensor(
                            out=kblk[:, b % 2, :].rearrange("p (h k) -> p h k", h=H),
                            in0=projT[:, 0, b * KEYS:(b + 1) * KEYS].unsqueeze(1).broadcast_to([P, H, KEYS]),
                            in1=m[:, :].unsqueeze(2).broadcast_to([P, H, KEYS]), op=ALU.mult).then_inc(S(f"kblk{layer}"), 1)
                        pool.wait_ge(S(f"kblk{layer}"), b + 1)
                elif ND[layer] == 16:
                    for c in range(2):
                        pool.wait_ge(S(f"projT{layer}"), c + 1)
                        for b in range(B):
                            pool.tensor_tensor(
                                out=A[:, b, 8 * c:8 * c + 8, :],
                                in0=projT[:, c, b * KEYS:(b + 1) * KEYS].unsqueeze(1).broadcast_to([P, 8, KEYS]),
                                in1=m[:, :].unsqueeze(2).broadcast_to([P, 8, KEYS]), op=ALU.mult).then_inc(S(f"kblk{layer}"), 1)
                            pool.wait_ge(S("kblk1"), B * c + b + 1)
                else:
                    for c in range(16):
                        pool.wait_ge(S(f"projT{layer}"), c + 1)
                        if c >= 2:
                            pool.wait_ge(S(f"kmm{layer}"), c - 1)
                        pool.tensor_tensor(
                            out=kblk[:, c % 2, 0:512].rearrange("p (b h k) -> p b h k", b=B, h=2),
                            in0=projT[:, c % 2, :].rearrange("p (b k) -> p b k", b=B).unsqueeze(2).broadcast_to([P, B, 2, KEYS]),
                            in1=m[:, :].unsqueeze(1).unsqueeze(3).broadcast_to([P, B, 2, KEYS]),
                            op=ALU.mult).then_inc(S(f"kblk{layer}"), 1)
                        pool.wait_ge(S("kblk3"), c + 1)

            def rsqrt(n):
                pool.wait_ge(S("ln_var"), n + 1)
                pool.tensor_tensor(out=rstd[:, :], in0=ve[:, :], in1=neghalf[:, :], op=ALU.pow).then_inc(S("ln_rstd"), 1)
                pool.wait_ge(S("ln_rstd"), n + 1)

            def clear_values(layer):
                n = ND[layer]
                v = vview(layer)
                if layer:
                    pool.wait_ge(S("attn_done"), layer)
                    chain(pool.memset(Vb[:, 0:B * PAIRS * 2 * (n + 1)], 0.0))
                chain(pool.memset(v[0:64, :, :, 0, n:n + 1], 1.0))
                pool.memset(v[64:128, :, :, 1, n:n + 1], 1.0).then_inc(S(f"vclear{layer}"), 1)
                pool.wait_ge(S(f"vclear{layer}"), 1)

            for layer in range(4):
                if layer in attn_layers:
                    if layer != 3:
                        clear_values(layer)
                    blocks(layer)
                    rsqrt(2 * layer)
                    if layer == 3:
                        def normalise(t, j, g):
                            pool.wait_ge(S("pden"), t + 1)
                            pool.tensor_tensor(out=pr[:, j], in0=pr[:, j],
                                               in1=rden[:, j, :].unsqueeze(2).broadcast_to([P, H, KEYS]),
                                               op=ALU.mult).then_inc(S("pnorm"), 1)
                            pool.wait_ge(S("pnorm"), t + 1)
                        with pool.Fori(0, T // 2) as i:
                            for j in range(2):
                                normalise(2 * i + j, j, None)
                if layer in route_layers():
                    rsqrt(2 * layer + 1)

        @block.tensor
        def _(pe):
            def prep(layer):
                pe.wait_ge(S("ctx_in"), 48)
                nd = ND[layer]
                if layer:
                    pe.wait_ge(S("banks_free"), layer)
                if layer in (0, 2):
                    w = aw0_sb if layer == 0 else aw2_sb
                    pe.wait_ge(S(f"aw{layer}_in"), 32)
                    pe.matmul(bank[0][:, 0:BK], w[:, 1, :], ctx_sb[:, :], start=True, stop=True).then_inc(S(f"proj{layer}"), 1)
                    for b in range(B):
                        pe.matmul(bank[1][:, b * D:(b + 1) * D], ctx_dup[:, b].rearrange("p s k -> p (s k)"), w[:, 2, :],
                                  start=True, stop=True).then_inc(S(f"vproj{layer}"), 1)
                    for b in range(B):
                        pe.wait_ge(S(f"kblk{layer}"), b + 1)
                        for c in range(2):
                            if b >= 2:
                                pe.wait_ge(S(f"a_sb{layer}"), 2 * (b - 2) + c + 1)
                            pe.matmul(bank[2 + 2 * (b % 2) + c][:, :], w[:, 0, :], kblk[:, b % 2, c * 512:(c + 1) * 512],
                                      start=True, stop=True).then_inc(S(f"kmm{layer}"), 1)
                elif layer == 1:
                    pe.wait_ge(S("fm2"), 1)
                    for c in range(2):
                        pe.matmul(bank[c][:, 0:BK], fm2[:, c].rearrange("p h s e -> p (h s e)"), ctx_sb[:, :],
                                  start=True, stop=True).then_inc(S("proj1"), 1)
                    for b in range(B):
                        pe.matmul(bank[2 + b][:, 0:256], ctx_dup[:, b].rearrange("p s k -> p (s k)"),
                                  fm2[:, :].rearrange("p c h s e -> p (c h s e)"), start=True, stop=True).then_inc(S("vproj1"), 1)
                else:
                    pe.wait_ge(S("aw3_in"), 16)

                    def proj(c):
                        if c >= 2:
                            pe.wait_ge(S("projT3"), c - 1)
                        w = aw3_sb[:, 1, c, :] if c < 8 else aw3_sb[:, 2, c - 8, :]
                        pe.matmul(bank[c % 2][:, 0:BK], w, ctx_sb[:, :], start=True, stop=True).then_inc(S("proj3"), 1)

                    proj(0)
                    for c in range(16):
                        if c + 1 < 16:
                            proj(c + 1)
                        pe.wait_ge(S("kblk3"), c + 1)
                        if c >= 2:
                            pe.wait_ge(S("a_sb3"), c - 1)
                        if c < 8:
                            mm = pe.matmul(bank[2 + c % 2][:, :], aw3_sb[:, 0, c, :], kblk[:, c % 2, 0:512], start=True, stop=True)
                        else:
                            for b in range(B):
                                mm = pe.matmul(bank[2 + c % 2][:, b * D:(b + 1) * D], kblk[:, c % 2, b * P:(b + 1) * P],
                                               aw3_sb[:, 3, c - 8, :], start=True, stop=True)
                        mm.then_inc(S("kmm3"), 1)

            def attention(layer):
                nd = ND[layer]
                G0 = 8 * layer
                if layer == 1:
                    pe.wait_ge(S("kblk1"), 8)
                    pe.wait_ge(S("v_sb1"), 8)
                elif layer == 3:
                    pe.wait_ge(S("a_sb3"), 16)
                else:
                    pe.wait_ge(S(f"a_sb{layer}"), 8)
                    pe.wait_ge(S(f"v_sb{layer}"), 8)

                def front(g, j, b):
                    pe.wait_ge(S("at_lg"), g + 1)
                    pe.wait_ge(S("at_xn"), g + 3)
                    pe.transpose(bank[2 * j][:, 0:P], xa[:, j, :], ident[:, :]).then_inc(S("at_xT"), 1)
                    pe.wait_ge(S("at_xTc"), g + 3)
                    if layer == 1:
                        for c in range(2):
                            mm = pe.matmul(bank[2 * j + 1][:, c * P:(c + 1) * P], fm2[:, c].rearrange("p h s e -> p (h s e)"),
                                           xaT[:, j, :], start=True, stop=True)
                        mm.then_inc(S("at_z"), 1)
                        pe.wait_ge(S("at_q"), g - G0 + 1)
                    for c in range(2):
                        lhs = qf[:, j, c, :] if layer == 1 else xaT[:, j, :]
                        mm = pe.matmul(bank[2 * j + c][:, :], lhs, A[:, b, 8 * c:8 * c + 8, :].rearrange("p h k -> p (h k)"),
                                       start=True, stop=True)
                    mm.then_inc(S("at_s"), 1)

                def turn(g, j):
                    if layer == 3:
                        pe.wait_ge(S("pnorm"), g - G0 + 1)
                    else:
                        pe.wait_ge(S("at_p"), g + 3)
                    for half in range(2):
                        pe.wait_ge(S("at_ptc"), 2 * g + 3 + half)
                        for q in range(4):
                            c = 4 * half + q
                            mm = pe.transpose(bank[4 + half][:, q * P:(q + 1) * P],
                                              pr[:, j, 2 * c:2 * c + 2, :].rearrange("p h k -> p (h k)"), ident[:, :])
                        mm.then_inc(S("at_pt"), 1)

                def values(g, j, b):
                    pe.wait_ge(S("at_res"), g + 1)
                    for half in range(2):
                        pe.wait_ge(S("at_ptc"), 2 * g + 5 + half)
                        for q in range(4):
                            c = 4 * half + q
                            lhs = PT[:, j, half, q * P:(q + 1) * P]
                            if layer == 3:
                                mm = pe.matmul(bank[6 + j][:, 0:D], lhs, VP3[:, b, c, :], start=(c == 0), stop=(c == PAIRS - 1))
                            else:
                                n = 2 * (nd + 1)
                                mm = pe.matmul(bank[6 + j][:, c * n:(c + 1) * n], lhs,
                                               vview(layer)[:, b, c].rearrange("p s n -> p (s n)"), start=True, stop=True)
                    mm.then_inc(S("at_o"), 1)

                def turn_out(g, j):
                    pe.wait_ge(S("at_on"), g + 3)
                    for c in range(nd // 8):
                        mm = pe.transpose(bank[6 + j][:, c * P:(c + 1) * P], on[:, j, c * P:(c + 1) * P], ident[:, :])
                    mm.then_inc(S("at_ot"), 1)

                def project(g, j):
                    pe.wait_ge(S("at_otc"), g + 3)
                    y = bank[6 + j][:, 256:256 + D]
                    if layer == 1:
                        for c in range(2):
                            pe.matmul(y, onT[:, j, c * P:(c + 1) * P], aw1_sb[:, c, :], start=(c == 0), stop=False)
                        mm = pe.matmul(y, ones_row[:, :], fcb_row[:, :], start=False, stop=True)
                    else:
                        w = aw0_sb if layer == 0 else aw2_sb
                        mm = pe.matmul(y, onT[:, j, 0:P], w[:, 3, :], start=True, stop=True)
                    mm.then_inc(S("at_y"), 1)

                def tile_step(g, j, b, ahead, first=False):
                    if ahead is not None:
                        front(g + 2, j, ahead)
                    turn(g, j)
                    if not first and layer != 3:
                        turn_out(g - 1, 1 - j)
                    values(g, j, b)
                    if not first and layer != 3:
                        project(g - 1, 1 - j)

                front(G0, 0, 0)
                front(G0 + 1, 1, 0)
                tile_step(G0, 0, 0, 1, first=True)
                with pe.Fori(0, T // 2 - 2) as i:
                    tile_step(2 * i + (G0 + 1), 1, i, i + 1)
                    tile_step(2 * i + (G0 + 2), 0, i + 1, i + 2)
                tile_step(G0 + T - 3, 1, B - 2, B - 1)
                tile_step(G0 + T - 2, 0, B - 1, None)
                tile_step(G0 + T - 1, 1, B - 1, None)
                if layer != 3:
                    turn_out(G0 + T - 1, 1)
                    project(G0 + T - 1, 1)

            def normed(layer):
                for t in range(T):
                    pe.wait_ge(S("f_xn"), T * layer + t + 1)
                    mm = pe.transpose(bank[t // 4][:, (t % 4) * P:(t % 4 + 1) * P], xn[:, t, :], ident[:, :])
                    if t % 4 == 3:
                        mm.then_inc(S("f_xT"), 1)
                pe.wait_ge(S("f_xTc"), 2 * (layer + 1))
                pe.wait_ge(S("wr_in"), 64)
                for t in range(T):
                    mm = pe.matmul(bank[2][:, t * E[layer]:(t + 1) * E[layer]], xnT[:, t * P:(t + 1) * P], wr_sb[layer][:, :],
                                   start=True, stop=True)
                mm.then_inc(S("router"), 1)
                pe.wait_ge(S("gates"), layer + 1)
                pe.transpose(bank[5][0:NP[layer], 0:P], rq[:, 0:NP[layer]], ident[:, :]).then_inc(S("gates_T"), 1)

            def search(layer):
                n = NP[layer]
                C0 = 15 * layer
                with pe.Fori(0, 15) as i:
                    pe.wait_ge(S("counted"), i + (C0 + 1))
                    pe.matmul(bank[4][:, 0:3], (same8 if E[layer] == 8 else same16)[0:n, :], cnt[0:n, :],
                              start=True, stop=True).then_inc(S("totals"), 1)
                pe.wait_ge(S("tie_counts"), layer + 1)
                pe.matmul(bank[4][0:n, 0:1], same(layer), tn[0:n, 0:1], start=True, stop=True)
                pe.matmul(bank[4][0:n, 1:2], before(layer), tn[0:n, 1:2], start=True, stop=True).then_inc(S("tie_totals"), 1)
                if layer == 1:
                    pe.wait_ge(S("sel_count"), 1)
                    pe.matmul(bank[4][0:n, 0:1], before(layer), tcol[0:n, 1:2], start=True, stop=True).then_inc(S("sel_before"), 1)
                    pe.wait_ge(S("gates_final"), 2)
                    pe.transpose(bank[5][:, 0:n], gfin[0:n, :], ident[:, :]).then_inc(S("slots_T"), 1)

            def open_sums():
                for c in range(2):
                    pe.matmul(bank[6 + c][:, :], zero_bf[:, 0:P], zero_bf[:, :], start=True, stop=False, skip_group_check=True)

            def add_out(layer):
                pe.wait_ge(S("f_yT"), 2 * (layer + 1))
                for t in range(T):
                    mm = pe.transpose(bank[t // 4][:, (t % 4) * P:(t % 4 + 1) * P],
                                      yT[:, t // 4, (t % 4) * P:(t % 4 + 1) * P], ident[:, :])
                    if t % 4 == 3:
                        mm.then_inc(S("f_out"), 1)

            def wslot(layer, u_in_body, i):
                return 16 * (i + (LOADS[layer][u_in_body] + 1))

            def gated_steps(layer, steps, q0, wg, wu, wd, src, flag):
                ns = len(steps)

                def up(s):
                    m, n, k = steps[s]
                    r = s % 2
                    pe.wait_ge(S(f"h{layer}"), q0 + (s + CREDIT - 1))
                    pe.matmul(bank[2 * r][0:k, :], wg(m), src[:, n * 512:(n + 1) * 512], start=True, stop=True)
                    pe.matmul(bank[2 * r + 1][0:k, :], wu(m), src[:, n * 512:(n + 1) * 512],
                              start=True, stop=True).then_inc(S(f"gu{layer}"), 1)

                def down(s):
                    m, n, k = steps[s]
                    pe.wait_ge(S(f"h{layer}"), q0 + (s + CREDIT + 1))
                    mm = pe.matmul(bank[6 + n][:, :], wd(m)[0:k, :], hh[0:k, s % 2, :], start=False, stop=flag and s >= ns - 1,
                                   skip_group_check=True)
                    mm.then_inc(S(f"down{layer}"), 1)
                return up, down

            def experts0():
                open_sums()

                def unit(i, j):
                    u = 2 * i + j
                    pe.wait_ge(S(f"w_in{j}"), wslot(0, j, i))
                    pe.wait_ge(S("gates_used0"), u + (CREDIT + 1))

                    def up(s):
                        n, m = divmod(s, 4)
                        pe.wait_ge(S("h0"), 8 * u + (s + 1))
                        pe.matmul(bank[s % 4][:, :], wring[:, j, m * P:(m + 1) * P], xg[:, j, n * 512:(n + 1) * 512],
                                  start=True, stop=True).then_inc(S("gu0"), 1)

                    def down(s):
                        n, m = divmod(s, 4)
                        pe.wait_ge(S("h0"), 8 * u + (s + 5))
                        mm = pe.matmul(bank[6 + n][:, :], wring[:, j, 512 + m * P:512 + (m + 1) * P], hh[:, s % 4, :],
                                       start=False, stop=False, skip_group_check=True)
                        mm.then_inc(S("down0"), 1)

                    for s in range(8):
                        up(s)
                        if s >= 2:
                            down(s - 2)
                    down(6)
                    down(7)

                with pe.Fori(0, 4) as i:
                    unit(i, 0)
                    unit(i, 1)

            def gated_experts(layer):
                open_sums()
                if layer == 2:
                    steps = [(0, n, P) for n in range(2)]
                else:
                    steps = [(m, n, F3_M[m]) for n in range(2) for m in range(3)]
                ns = len(steps)
                w = wring

                def views(j):
                    if layer == 2:
                        return (lambda m: w[:, j, 0:P], lambda m: w[:, j, P:2 * P], lambda m: w[:, j, 2 * P:3 * P])
                    return (lambda m: w[:, j, m * P:m * P + F3_M[m]], lambda m: w[:, j, 352 + m * P:352 + m * P + F3_M[m]],
                            lambda m: w[:, j, 704 + m * P:704 + (m + 1) * P])

                q1 = 0
                if layer == 2:
                    pe.wait_ge(S("sh_in"), 32)
                    up, down = gated_steps(2, steps, 0, lambda m: sh2_sb[:, 0, :], lambda m: sh2_sb[:, 1, :],
                                           lambda m: sh2_sb[:, 2, :], xnT, False)
                    up(0)
                    up(1)
                    down(0)
                    down(1)
                    q1 = 2
                with pe.Fori(0, 4) as i:
                    pend = None
                    for j in range(2):
                        u = 2 * i + j
                        q0 = (2 * i + j) * ns + q1
                        pe.wait_ge(S(f"w_in{j}"), wslot(layer, j, i))
                        if layer == 3:
                            pe.wait_ge(S("gates_used3"), u + (CREDIT + 1))
                        src = xnT if layer == 2 else xg[:, j, :]
                        up, down = gated_steps(layer, steps, q0, *views(j), src, False)
                        for s in range(ns):
                            up(s)
                            if s >= 1:
                                down(s - 1)
                            elif pend:
                                pend(ns - 1)
                        pend = down
                    pend(ns - 1)

            def experts1():
                open_sums()
                steps = [(m, n, P) for n in range(2) for m in range(2)]
                pe.wait_ge(S("sh_in"), 32)
                up, down = gated_steps(1, steps, 0, lambda m: sh1_sb[:, m, :], lambda m: sh1_sb[:, 2 + m, :],
                                       lambda m: sh1_sb[:, 4 + m, :], xnT, False)
                for s in range(4):
                    up(s)
                    if s:
                        down(s - 1)
                down(3)
                Q1 = 4

                def gather(i, r):
                    pe.wait_ge(S("onehot"), 8 * i + 8)
                    pe.wait_ge(S("xgc"), i + 1)
                    for t in range(T):
                        for k in range(3):
                            mm = pe.matmul(bank[4][:, :], xs[:, k, t, :], P4[r][:, t].rearrange("p e c -> p (e c)"),
                                           start=(t == 0 and k == 0), stop=(t == T - 1 and k == 2))
                    mm.then_inc(S("xg_mm"), 1)

                def up1(u, j):
                    r = j % 2
                    q = u + Q1
                    pe.wait_ge(S(f"w_in{j}"), 0 + W_OF(u, j))
                    pe.wait_ge(S("h1"), q + (CREDIT - 1))
                    for m in range(4):
                        pe.matmul(bank[2 * r][:, m * P:(m + 1) * P], wring[:, j, m * P:(m + 1) * P], xgT[:, j, :],
                                  start=True, stop=True)
                    for m in range(4):
                        mm = pe.matmul(bank[2 * r + 1][:, m * P:(m + 1) * P], wring[:, j, 512 + m * P:512 + (m + 1) * P],
                                       xgT[:, j, :], start=True, stop=True)
                    mm.then_inc(S("gu1"), 1)

                def down1(i, r, u, j):
                    pe.wait_ge(S("eo"), u + 1)
                    for t in range(T):
                        pe.matmul(bank[5][:, P:P + 3], P4[r][:, t, j, :], ps[:, t, 4 * i + j, :], start=(t == 0), stop=(t == T - 1))
                    pe.wait_ge(S("h1"), u + (Q1 + CREDIT + 1))
                    for m in range(4):
                        mm = pe.matmul(bank[5][:, 0:P], hh[:, j % 2, m * P:(m + 1) * P], wring[:, j, 1024 + m * P:1024 + (m + 1) * P],
                                       start=(m == 0), stop=(m == 3))
                    mm.then_inc(S("down1"), 1)

                def scatter(u, j):
                    pe.wait_ge(S("eo"), u + 2)
                    pe.wait_ge(S("gates_used1"), u + (CREDIT + 1))
                    for n in range(2):
                        mm = pe.matmul(bank[6 + n][:, :], eo[:, j % 2, :], PTs[:, j % 2, n * 512:(n + 1) * 512],
                                       start=False, stop=False, skip_group_check=True)
                    mm.then_inc(S("scattered"), 1)

                W_OF_I = [None]

                def W_OF(u, j):
                    return 16 * (W_OF_I[0] + (LOADS[1][j] + 1))

                with pe.Fori(0, 2) as half:
                    for r in range(2):
                        i = 2 * half + r
                        W_OF_I[0] = i
                        gather(i, r)
                        pe.wait_ge(S("xgc"), i + 2)
                        for j in range(4):
                            up1(4 * i + j, j)
                            if j >= 1:
                                down1(i, r, 4 * i + (j - 1), j - 1)
                            if j >= 2:
                                scatter(4 * i + (j - 2), j - 2)
                        down1(i, r, 4 * i + 3, 3)
                        scatter(4 * i + 2, 2)
                        scatter(4 * i + 3, 3)

            def close_sums(layer):
                for c in range(2):
                    mm = pe.matmul(bank[6 + c][:, :], zero_bf[:, 0:P], zero_bf[:, :], start=False, stop=True, skip_group_check=True)
                    mm.then_inc(S("f_sum"), 1)

            pe.wait_ge(S("const"), 1)
            for layer in range(4):
                if layer in attn_layers:
                    prep(layer)
                    attention(layer)
                if layer in route_layers():
                    pe.wait_ge(S("banks_free_a"), layer + 1)
                    normed(layer)
                    if layer < 2:
                        search(layer)
                    if layer == 0:
                        experts0()
                    elif layer == 1:
                        experts1()
                    else:
                        gated_experts(layer)
                    close_sums(layer)
                    add_out(layer)

        @block.scalar
        def _(act):
            def copy(dst, src):
                return act.activation(dst, src, ACT.Copy)

            def prep(layer):
                nd = ND[layer]
                if layer in (0, 2):
                    act.wait_ge(S(f"proj{layer}"), 1)
                    if layer:
                        act.wait_ge(S("attn_done"), layer)
                    copy(projT[:, 0, :], bank[0][:, 0:BK]).then_inc(S(f"projT{layer}"), 1)
                    act.wait_ge(S(f"vclear{layer}"), 1)
                    act.wait_ge(S(f"vproj{layer}"), B)
                    v = vview(layer)
                    for b in range(B):
                        src = bank[1][:, b * D:(b + 1) * D].rearrange("p (c s n) -> p c s n", c=PAIRS, s=2)
                        for s in range(2):
                            copy(v[64 * s:64 * s + 64, b, :, s, 0:nd], src[64 * s:64 * s + 64, :, s, :]).then_inc(S(f"v_sb{layer}"), 1)
                    for b in range(B):
                        for c in range(2):
                            act.wait_ge(S(f"kmm{layer}"), 2 * b + c + 1)
                            copy(A[:, b, 8 * c:8 * c + 8, :], bank[2 + 2 * (b % 2) + c][:, :].rearrange("p (h k) -> p h k", h=8)
                                 ).then_inc(S(f"a_sb{layer}"), 1)
                elif layer == 1:
                    act.wait_ge(S("bias_col"), 1)
                    act.wait_ge(S("attn_done"), 1)
                    for c in range(2):
                        act.wait_ge(S("proj1"), c + 1)
                        act.activation(projT[:, c, :], bank[c][:, 0:BK], ACT.Exp, bias=bias_col[:, 0:1]).then_inc(S("projT1"), 1)
                    act.wait_ge(S("vclear1"), 1)
                    act.wait_ge(S("vbias"), B)
                    v = vview(1)
                    for b in range(B):
                        src = kblk[:, b // 2, (b % 2) * 512:(b % 2) * 512 + 256].rearrange("p (c s n) -> p c s n", c=PAIRS, s=2)
                        for s in range(2):
                            act.activation(v[64 * s:64 * s + 64, b, :, s, 0:nd], src[64 * s:64 * s + 64, :, s, :],
                                           ACT.Exp).then_inc(S("v_sb1"), 1)
                else:
                    act.wait_ge(S("attn_done"), 3)

                    def proj_out(c):
                        act.wait_ge(S("proj3"), c + 1)
                        if c >= 2:
                            act.wait_ge(S("kblk3"), c - 1)
                        copy(projT[:, c % 2, :], bank[c % 2][:, 0:BK]).then_inc(S("projT3"), 1)

                    proj_out(0)
                    for c in range(16):
                        if c + 1 < 16:
                            proj_out(c + 1)
                        act.wait_ge(S("kmm3"), c + 1)
                        if c < 8:
                            dst = A[:, :, 2 * c:2 * c + 2, :]
                            src = bank[2 + c % 2][:, :].rearrange("p (b h k) -> p b h k", b=B, h=2)
                        else:
                            dst = VP3[:, :, c - 8, :]
                            src = bank[2 + c % 2][:, :].rearrange("p (b n) -> p b n", b=B)
                        copy(dst, src).then_inc(S("a_sb3"), 1)

            def attention(layer):
                nd = ND[layer]
                G0 = 8 * layer

                def x_out(g, j):
                    act.wait_ge(S("at_s"), g + 1)
                    act.wait_ge(S("at_xT"), g + 3)
                    copy(xaT[:, j, :], bank[2 * j][:, 0:P]).then_inc(S("at_xTc"), 1)
                    if layer == 1:
                        act.wait_ge(S("at_z"), g - G0 + 1)
                        act.activation(qf[:, j, :, :], bank[2 * j + 1][:, 0:256].rearrange("p (c q) -> p c q", c=2), ACT.Exp,
                                       bias=bias_col[:, 0:1]).then_inc(S("at_q"), 1)

                def exp(g, j):
                    act.wait_ge(S("at_lg"), g + 3)
                    act.wait_ge(S("at_pt"), 2 * g + 2)
                    act.activation(pr[:, j], lg[:, j], ACT.Exp, scale=(1.0 if layer == 0 else SCALE[layer])).then_inc(S("at_p"), 1)

                def turned(g, j):
                    act.wait_ge(S("at_o"), g + 1)
                    for half in range(2):
                        act.wait_ge(S("at_pt"), 2 * g + 5 + half)
                        copy(PT[:, j, half, :], bank[4 + half][:, :]).then_inc(S("at_ptc"), 1)

                def out_turned(g, j):
                    act.wait_ge(S("at_y"), g + 1)
                    act.wait_ge(S("at_ot"), g + 3)
                    n = 16 * nd
                    copy(onT[:, j, 0:n], bank[6 + j][:, 0:n]).then_inc(S("at_otc"), 1)

                def tile_step(g, j, first=False, ahead=True, last=False):
                    if ahead:
                        x_out(g + 2, j)
                    turned(g, j)
                    if not first and layer != 3:
                        out_turned(g - 1, 1 - j)
                    if not last:
                        exp(g + 1, 1 - j)

                x_out(G0, 0)
                x_out(G0 + 1, 1)
                exp(G0, 0)
                tile_step(G0, 0, first=True)
                with act.Fori(0, T // 2 - 2) as i:
                    tile_step(2 * i + (G0 + 1), 1)
                    tile_step(2 * i + (G0 + 2), 0)
                tile_step(G0 + T - 3, 1)
                tile_step(G0 + T - 2, 0, ahead=False)
                tile_step(G0 + T - 1, 1, ahead=False, last=True)
                if layer != 3:
                    out_turned(G0 + T - 1, 1)

            def normed(layer):
                for c in range(2):
                    act.wait_ge(S("f_xT"), 2 * layer + c + 1)
                    copy(xnT[:, c * 512:(c + 1) * 512], bank[c][:, :]).then_inc(S("f_xTc"), 1)
                if layer < 3:
                    act.wait_ge(S("r_shift"), layer + 1)
                    act.activation(rl[:, 0:NP[layer]], rp[:, 0:NP[layer]], ACT.Exp).then_inc(S("r_exp"), 1)

            def gated(layer, func, q, s, k):
                act.wait_ge(S(f"h{layer}"), q + (CREDIT - 1))
                act.wait_ge(S(f"gu{layer}"), q + (1 + 2 * UPS.get(layer, 0)))
                act.activation(sg[0:k, s % 2, :], bank[2 * (s % 2)][0:k, :], func).then_inc(S(f"sg{layer}"), 1)

            def experts0():
                with act.Fori(0, 8) as u:
                    for s in range(8):
                        act.wait_ge(S("gu0"), 8 * u + (s + 1 + 2 * UPS[0]))
                        act.wait_ge(S("down0"), 8 * u + (s + 1))
                        act.activation(hh[:, s % 4, :], bank[s % 4][:, :], ACT.Relu).then_inc(S("h0"), 1)

            def experts1():
                for s in range(4):
                    gated(1, ACT.Gelu, s, s, P)
                with act.Fori(0, 4) as i:
                    act.wait_ge(S("xg_mm"), i + 1)
                    act.wait_ge(S("gu1"), 4 * i + 4)
                    copy(xgT[:, :, :], bank[4][:, :].rearrange("p (e c) -> p e c", e=4)).then_inc(S("xgc"), 1)
                    for j in range(4):
                        gated(1, ACT.Gelu, 4 * i + (j + 4), j, P)

            def gated_experts(layer):
                q1 = 0
                if layer == 2:
                    for s in range(2):
                        gated(2, ACT.Silu, s, s, P)
                    q1 = 2
                ks = [P, P] if layer == 2 else F3_M + F3_M
                with act.Fori(0, 8) as u:
                    for s, k in enumerate(ks):
                        gated(layer, ACT.Silu, len(ks) * u + (s + q1), s, k)

            def add_out(layer):
                for c in range(2):
                    act.wait_ge(S("f_sum"), 2 * (layer + 1))
                    copy(yT[:, c, :], bank[6 + c][:, :]).then_inc(S("f_yT"), 1)

            for name, n in (("at_s", 2), ("at_pt", 4), ("at_o", 2), ("at_y", 2), ("at_z", 0)):
                if n:
                    act.sem_inc(S(name), n)
            act.wait_ge(S("const"), 1)
            for layer in range(4):
                if layer in attn_layers:
                    prep(layer)
                    attention(layer)
                if layer in route_layers():
                    normed(layer)
                    if layer == 0:
                        experts0()
                    elif layer == 1:
                        experts1()
                    else:
                        gated_experts(layer)
                    add_out(layer)

        @block.vector
        def _(dve):
            step = [0]

            def chain(ins):
                ins.then_inc(S("dve_step"), 1)
                step[0] += 1
                dve.wait_ge(S("dve_step"), step[0])

            def stats(n):
                for t in range(T):
                    dve.bn_stats(st6[:, t, :], x[:, t, :]).then_inc(S("dve_step"), 1)
                step[0] += T
                dve.wait_ge(S("dve_step"), step[0])
                for t in range(T):
                    dve.bn_aggr(mv[:, t, :], st6[:, t, :]).then_inc(S("dve_step"), 1)
                step[0] += T
                dve.wait_ge(S("dve_step"), step[0])
                dve.tensor_scalar(ve[:, :], mv[:, :, 1], EPS, None, ALU.add).then_inc(S("ln_var"), 1)
                dve.wait_ge(S("ln_rstd"), n + 1)

            def setup():
                dve.tensor_scalar(mod_a[:, 0:1], chan_i[:, :], 7, None, ALU.bitwise_and)
                dve.tensor_scalar(mod_a[:, 1:2], chan_i[:, :], 15, None, ALU.bitwise_and)
                dve.tensor_scalar(sgn_i[:, :], chan_i[:, :], 3, 1, ALU.logical_shift_right, ALU.bitwise_and)
                dve.tensor_scalar(mod_r[:, 1, :], mod_r[:, 0, :], 15, None, ALU.bitwise_and)
                chain(dve.tensor_scalar(mod_rf[:, 0, :], iota_row[:, :], iota_col[:, 0:1], None, ALU.is_gt))
                chain(dve.tensor_scalar(mod_r[:, 0, :], mod_r[:, 0, :], 7, None, ALU.bitwise_and))
                chain(dve.tensor_copy(mod_f[:, :], mod_a[:, :]))
                dve.tensor_scalar(sgn[:, :], sgn_i[:, :], -2.0, 1.0, ALU.mult, ALU.add)
                dve.tensor_scalar(same8[:, :], mod_r[:, 0, :], mod_f[:, 0:1], None, ALU.is_equal)
                chain(dve.tensor_scalar(same16[:, :], mod_r[:, 1, :], mod_f[:, 1:2], None, ALU.is_equal))
                dve.tensor_tensor(before8[:, :], same8[:, :], mod_rf[:, 0, :], ALU.mult)
                chain(dve.tensor_tensor(before16[:, :], same16[:, :], mod_rf[:, 0, :], ALU.mult))
                dve.wait_ge(S("aw1_in"), 64)
                dve.tensor_tensor(bias_col[:, :], fmrep[:, 8:9], sgn[:, :], ALU.mult).then_inc(S("bias_col"), 1)
                for c in range(2):
                    m = hm8[:, 8 * c:8 * c + 8].unsqueeze(2).broadcast_to([P, 8, 8])
                    w = fmrep[:, 0:8].unsqueeze(1).broadcast_to([P, 8, 8])
                    dve.tensor_tensor(fm2[:, c, :, 0, :], w, m, ALU.mult)
                    mm = dve.scalar_tensor_tensor(out=fm2[:, c, :, 1, :], in0=w, scalar=-1.0, in1=m, op0=ALU.mult, op1=ALU.mult)
                mm.then_inc(S("fm2"), 1)
                dve.wait_ge(S("aw2_in"), 32)
                chain(dve.tensor_copy(qm[:, :], qm8[:, :]))

            def value_bias():
                dve.wait_ge(S("attn_done"), 1)
                for b in range(B):
                    dve.wait_ge(S("vproj1"), b + 1)
                    src = bank[2 + b][:, 0:256].rearrange("p (h s e) -> p h s e", h=H, s=2)
                    dst = kblk[:, b // 2, (b % 2) * 512:(b % 2) * 512 + 256].rearrange("p (h s e) -> p h s e", h=H, s=2)
                    bb = fmb_all[:, :].unsqueeze(1).broadcast_to([P, H, 8])
                    dve.tensor_tensor(dst[:, :, 0, :], src[:, :, 0, :], bb, ALU.add)
                    dve.tensor_tensor(dst[:, :, 1, :], src[:, :, 1, :], bb, ALU.subtract).then_inc(S("vbias"), 1)

            def attention(layer):
                nd = ND[layer]
                G0 = 8 * layer
                base = step[0]
                per = {0: 3, 1: 3, 2: 2, 3: 2}[layer]

                def norm_x(g, j, t):
                    dve.wait_ge(S("at_xT"), g + 1)
                    dve.tensor_scalar(xa[:, j, :], x[:, t, :], mv[:, t, 0:1], rstd[:, bass.ds(t, 1)], ALU.subtract,
                                      ALU.mult).then_inc(S("at_xn"), 1)

                def softmax_in(g, j):
                    sc = [bank[2 * j + c][:, :].rearrange("p (h k) -> p h k", h=8) for c in range(2)]
                    dve.wait_ge(S("at_s"), g + 3)
                    dve.wait_ge(S("at_p"), g + 1)
                    if layer == 2:
                        lim = CLIP / SCALE[2]
                        for c in range(2):
                            mm = dve.tensor_scalar(lg[:, j, 8 * c:8 * c + 8, :], sc[c], lim, -lim, ALU.min, ALU.max)
                        mm.then_inc(S("at_lg"), 1)
                        return
                    if layer == 0:
                        for c in range(2):
                            mm = dve.scalar_tensor_tensor(
                                out=lg[:, j, 8 * c:8 * c + 8, :], in0=sc[c], scalar=SCALE[0],
                                in1=fside_sb[:, j, :].unsqueeze(1).broadcast_to([P, 8, KEYS]), op0=ALU.mult, op1=ALU.add)
                            mm.then_inc(S("lg_raw"), 1)
                        dve.wait_ge(S("lg_raw"), 2 * g + 2)
                        sc = [lg[:, j, 8 * c:8 * c + 8, :] for c in range(2)]
                    for c in range(2):
                        dve.tensor_reduce(mx[:, j, 8 * c:8 * c + 8], sc[c], AX.X, ALU.max).then_inc(S("at_mx"), 1)
                    dve.wait_ge(S("at_mx"), 2 * MXI(g) + 2)
                    for c in range(2):
                        mm = dve.tensor_tensor(lg[:, j, 8 * c:8 * c + 8, :], sc[c],
                                               mx[:, j, 8 * c:8 * c + 8].unsqueeze(2).broadcast_to([P, 8, KEYS]), ALU.subtract)
                    mm.then_inc(S("at_lg"), 1)

                def MXI(g):
                    return g if layer < 2 else g - 8

                def den(g, j):
                    dve.wait_ge(S("at_p"), g + 3)
                    dve.tensor_reduce(rden2[:, j, :], pr[:, j], AX.X, ALU.add).then_inc(S("psum"), 1)
                    dve.wait_ge(S("psum"), g - G0 + 1)
                    dve.reciprocal(rden[:, j, :], rden2[:, j, :]).then_inc(S("pden"), 1)

                def norm_out(g, j, t):
                    n = nd + 1
                    o = bank[6 + j][:, 0:H * n].rearrange("p (h n) -> p h n", h=H)
                    dve.wait_ge(S("at_o"), g + 3)
                    dve.reciprocal(rden[:, j, :], o[:, :, nd]).then_inc(S("at_rd"), 1)
                    dve.wait_ge(S("at_rd"), g + 1)
                    r = rden
                    if layer == 2:
                        dve.tensor_scalar(rden2[:, j, :], rden[:, j, :], qm[:, bass.ds(t, 1)], None, ALU.mult).then_inc(S("at_rm"), 1)
                        dve.wait_ge(S("at_rm"), g - G0 + 1)
                        r = rden2
                    dve.wait_ge(S("at_ot"), g + 1)
                    dve.tensor_tensor(on[:, j, 0:H * nd].rearrange("p (h n) -> p h n", h=H), o[:, :, 0:nd],
                                      r[:, j, :].unsqueeze(2).broadcast_to([P, H, nd]), ALU.mult).then_inc(S("at_on"), 1)

                def residual(g, j, t):
                    if layer == 3:
                        dve.wait_ge(S("at_o"), g + 3)
                        y = bank[6 + j][:, 0:D]
                    else:
                        dve.wait_ge(S("at_y"), g + 3)
                        y = bank[6 + j][:, 256:256 + D]
                    dve.tensor_tensor(x[:, t, :], y, x[:, t, :], ALU.add).then_inc(S("at_res"), 1)

                def tile_step(t, j, first=False, ahead=True, last=False):
                    g = t + G0
                    if ahead:
                        norm_x(g + 2, j, t + 2)
                    if layer == 3:
                        den(g, j)
                    elif not first:
                        norm_out(g - 1, 1 - j, t - 1)
                    if not last:
                        softmax_in(g + 1, 1 - j)
                    if not first:
                        residual(g - 1, 1 - j, t - 1)

                norm_x(G0, 0, 0)
                norm_x(G0 + 1, 1, 1)
                softmax_in(G0, 0)
                tile_step(0, 0, first=True)
                with dve.Fori(0, T // 2 - 2) as i:
                    tile_step(2 * i + 1, 1)
                    tile_step(2 * i + 2, 0)
                tile_step(T - 3, 1)
                tile_step(T - 2, 0, ahead=False)
                tile_step(T - 1, 1, ahead=False, last=True)
                if layer != 3:
                    norm_out(G0 + T - 1, 1, T - 1)
                residual(G0 + T - 1, 1, T - 1)
                dve.wait_ge(S("at_res"), G0 + T + CREDIT)

            def ev(t, layer):
                return t[:, 0:NP[layer]].rearrange("p (t e) -> p t e", t=T)

            def onehot_of_max(layer, src, dst):
                e = E[layer]
                chain(dve.tensor_reduce(rm[:, :], src, AX.X, ALU.max))
                chain(dve.tensor_tensor(ev(rk, layer), src, rm[:, :].unsqueeze(2).broadcast_to([P, T, e]), ALU.is_equal))
                chain(dve.tensor_tensor(ev(rk, layer), ev(rk, layer), rev[:, 0:e].unsqueeze(1).broadcast_to([P, T, e]), ALU.mult))
                chain(dve.tensor_reduce(rm[:, :], ev(rk, layer), AX.X, ALU.max))
                chain(dve.tensor_tensor(dst, ev(rk, layer), rm[:, :].unsqueeze(2).broadcast_to([P, T, e]), ALU.is_equal))

            def route(layer):
                n, e = NP[layer], E[layer]
                for t in range(T):
                    dve.tensor_scalar(xn[:, t, :], x[:, t, :], mv[:, t, 0:1], rstd[:, t:t + 1], ALU.subtract,
                                      ALU.mult).then_inc(S("f_xn"), 1)
                if layer == 1:
                    dve.wait_ge(S("f_xn"), T * 2)
                    split(xn[:, :, :], xres[:, :, :], [xs[:, k] for k in range(3)])
                dve.wait_ge(S("router"), layer + 1)
                z = bank[2][:, 0:n].rearrange("p (t e) -> p t e", t=T)
                if layer == 3:
                    chain(dve.tensor_copy(ev(rp, 3), z))
                    onehot_of_max(3, ev(rp, 3), ev(rq, 3))
                else:
                    chain(dve.tensor_reduce(rm[:, :], z, AX.X, ALU.max))
                    dve.tensor_tensor(ev(rp, layer), z, rm[:, :].unsqueeze(2).broadcast_to([P, T, e]), ALU.subtract).then_inc(S("r_shift"), 1)
                    dve.wait_ge(S("r_exp"), layer + 1)
                    chain(dve.tensor_reduce(rr[:, :], ev(rl, layer), AX.X, ALU.add))
                    chain(dve.reciprocal(rm[:, :], rr[:, :]))
                    prob = ev(rq if layer == 1 else rp, layer)
                    chain(dve.tensor_tensor(prob, ev(rl, layer), rm[:, :].unsqueeze(2).broadcast_to([P, T, e]), ALU.mult))
                    if layer != 1:
                        onehot_of_max(layer, prob, ev(r1, layer))
                        chain(dve.scalar_tensor_tensor(out=r2[:, 0:n], in0=r1[:, 0:n], scalar=-4.0, in1=rp[:, 0:n], op0=ALU.mult, op1=ALU.add))
                        onehot_of_max(layer, ev(r2, layer), ev(rq, layer))
                        chain(dve.tensor_tensor(r1[:, 0:n], r1[:, 0:n], rq[:, 0:n], ALU.add))
                        chain(dve.tensor_tensor(rq[:, 0:n], r1[:, 0:n], rp[:, 0:n], ALU.mult))
                dve.sem_inc(S("gates"), 1)
                dve.wait_ge(S("gates_T"), layer + 1)
                if layer == 1:
                    split(ev(rq, 1), pres[:, :, :], [ps[:, :, :, k] for k in range(3)])
                if layer < 2:
                    chain(dve.tensor_copy(gts[0:n, :], bank[5][0:n, 0:P]))
                    search(layer)
                else:
                    dve.wait_ge(S("gates_out"), 16 * layer)
                    dve.tensor_copy(gfin[0:n, :], bank[5][0:n, 0:P]).then_inc(S("gates_final"), 1)

            def split(src, rest, parts):
                chain(dve.tensor_copy(parts[0], src))
                chain(dve.tensor_tensor(rest, src, parts[0], ALU.subtract))
                chain(dve.tensor_copy(parts[1], rest))
                chain(dve.tensor_tensor(rest, rest, parts[1], ALU.subtract))
                chain(dve.tensor_copy(parts[2], rest))

            def search(layer):
                n = NP[layer]
                cap = float(CAP[layer])
                dve.memset(cur[:, :], 0)
                for k in range(3):
                    ins = dve.memset(stp[:, k:k + 1], (k + 1) << 28)
                chain(ins)
                base = step[0]
                with dve.Fori(0, 15) as i:
                    s0 = 7 * i + base
                    dve.tensor_tensor(cand[0:n, :], stp[0:n, :], cur[0:n, 0:1].broadcast_to([n, 3]), ALU.bitwise_or
                                      ).then_inc(S("dve_step"), 1)
                    dve.wait_ge(S("dve_step"), s0 + 1)
                    for k in range(3):
                        ins = dve.tensor_scalar(junk[0:n, :], gts[0:n, :], cand[0:n, k:k + 1].bitcast(F32), None, ALU.is_ge,
                                                ALU.add, accum_out=cnt[0:n, k:k + 1])
                        if k < 2:
                            ins.then_inc(S("dve_step"), 1)
                            dve.wait_ge(S("dve_step"), s0 + (k + 2))
                    ins.then_inc(S("counted"), 1)
                    dve.wait_ge(S("totals"), i + (15 * layer + 1))
                    dve.tensor_scalar(junk3[0:n, :], bank[4][0:n, 0:3], cap, None, ALU.is_ge, ALU.add,
                                      accum_out=nsat[0:n, :]).then_inc(S("dve_step"), 1)
                    dve.wait_ge(S("dve_step"), s0 + 4)
                    dve.tensor_tensor(addb[0:n, :], nsat[0:n, :], stp[0:n, 0:1], ALU.mult).then_inc(S("dve_step"), 1)
                    dve.wait_ge(S("dve_step"), s0 + 5)
                    dve.tensor_tensor(cur[0:n, :], cur[0:n, :], addb[0:n, :], ALU.bitwise_or).then_inc(S("dve_step"), 1)
                    dve.wait_ge(S("dve_step"), s0 + 6)
                    dve.tensor_scalar(stp[0:n, :], stp[0:n, :], 2, None, ALU.logical_shift_right).then_inc(S("dve_step"), 1)
                    dve.wait_ge(S("dve_step"), s0 + 7)
                step[0] += 7 * 15
                thr = cur[0:n, 0:1].bitcast(F32)
                dve.tensor_scalar(tgt[0:n, :], gts[0:n, :], thr, None, ALU.is_gt, ALU.add, accum_out=tn[0:n, 0:1])
                dve.tensor_scalar(teq[0:n, :], gts[0:n, :], thr, None, ALU.is_equal, ALU.add, accum_out=tn[0:n, 1:2]
                                  ).then_inc(S("tie_counts"), 1)
                dve.wait_ge(S("tie_totals"), layer + 1)
                chain(dve.tensor_scalar(tcol[0:n, 0:1], bank[4][0:n, 0:1], -1.0, cap, ALU.mult, ALU.add))
                chain(dve.tensor_copy(tcol[0:n, 2:3], bank[4][0:n, 1:2]))
                chain(dve.tensor_tensor_scan(tcum[0:n, :], teq[0:n, :], zrow[0:n, :], tcol[0:n, 2:3], ALU.add, ALU.add))
                chain(dve.scalar_tensor_tensor(out=tsel[0:n, :], in0=tcum[0:n, :], scalar=tcol[0:n, 0:1], in1=teq[0:n, :],
                                               op0=ALU.is_le, op1=ALU.mult))
                if layer == 0:
                    chain(dve.tensor_tensor(tsel[0:n, :], tsel[0:n, :], tgt[0:n, :], ALU.add))
                    dve.tensor_tensor(gfin[0:n, :], tsel[0:n, :], gts[0:n, :], ALU.mult).then_inc(S("gates_final"), 1)
                    return
                chain(dve.tensor_tensor(tsel[0:n, :], tsel[0:n, :], tgt[0:n, :], ALU.add))
                dve.tensor_reduce(tcol[0:n, 1:2], tsel[0:n, :], AX.X, ALU.add).then_inc(S("sel_count"), 1)
                dve.wait_ge(S("sel_before"), 1)
                chain(dve.tensor_copy(tcol[0:n, 3:4], bank[4][0:n, 0:1]))
                chain(dve.tensor_tensor_scan(tcum[0:n, :], tsel[0:n, :], zrow[0:n, :], tcol[0:n, 3:4], ALU.add, ALU.add))
                chain(dve.tensor_tensor(tcum[0:n, :], tcum[0:n, :], tsel[0:n, :], ALU.mult))
                dve.wait_ge(S("gates_out"), 16)
                dve.tensor_scalar(gfin[0:n, :], tcum[0:n, :], -1.0, None, ALU.add).then_inc(S("gates_final"), 1)
                dve.wait_ge(S("slots_T"), 1)
                chain(dve.tensor_copy(slotc[:, 0:n], bank[5][:, 0:n]))

            def gate_tokens(layer, i, j):
                u = 2 * i + j
                dve.wait_ge(S(f"gb_in{j}"), 16 * (i + (GB0[layer] + 1)))
                dve.wait_ge(S(f"gu{layer}"), UPS[layer] * u + UPS[layer])
                dve.tensor_tensor(xg[:, j, :], xnT[:, :], gb[:, j, :], ALU.mult).then_inc(S(f"gates_used{layer}"), 1)

            GB0 = [0, 4, 12, 20]

            def product(layer, q, s, k, gate=None):
                dve.wait_ge(S(f"down{layer}"), q + 1)
                dve.wait_ge(S(f"sg{layer}"), q + 1)
                r = s % 2
                if gate is None:
                    dve.tensor_tensor(hh[0:k, r, :], bank[2 * r + 1][0:k, :], sg[0:k, r, :], ALU.mult).then_inc(S(f"h{layer}"), 1)
                else:
                    dve.tensor_tensor(hh[0:k, 2 + r, :], bank[2 * r + 1][0:k, :], gate, ALU.mult).then_inc(S("hg"), 1)
                    dve.wait_ge(S("hg"), q - 1)
                    dve.tensor_tensor(hh[0:k, r, :], hh[0:k, 2 + r, :], sg[0:k, r, :], ALU.mult).then_inc(S(f"h{layer}"), 1)

            def experts0():
                with dve.Fori(0, 4) as i:
                    for j in range(2):
                        gate_tokens(0, i, j)

            def experts1():
                def onehots(i, r, tiles):
                    for t in tiles:
                        dve.tensor_tensor(P4[r][:, t], iota_row[:, :].unsqueeze(1).broadcast_to([P, 4, P]),
                                          slotc[:, bass.ds(4 * i + t * 16, 4)].unsqueeze(2).broadcast_to([P, 4, P]),
                                          ALU.is_equal).then_inc(S("onehot"), 1)

                def placed(i, j, u, s):
                    dve.wait_ge(S(f"gb_in{j % 2}"), 16 * (2 * i + (GB0[1] + j // 2 + 1)))
                    dve.wait_ge(S("scattered"), u + 1)
                    dve.tensor_scalar(PTs[:, j % 2, :], gb[:, j % 2, :], iota_col[:, 0:1], None, ALU.is_equal
                                      ).then_inc(S("gates_used1"), 1)

                def weigh(u, j):
                    dve.wait_ge(S("down1"), u + (4 + 2 + 1))
                    chain_in(dve.tensor_reduce(wcol[:, j % 2:j % 2 + 1], bank[5][:, P:P + 3], AX.X, ALU.add), u)
                    dve.wait_ge(S("scattered"), u + 1)
                    dve.tensor_scalar(eo[:, j % 2, :], bank[5][:, 0:P], wcol[:, j % 2:j % 2 + 1], None, ALU.mult).then_inc(S("eo"), 1)

                def chain_in(ins, u):
                    ins.then_inc(S("weight"), 1)
                    dve.wait_ge(S("weight"), u + 1)

                onehots(0, 0, range(T))
                for s in range(4):
                    product(1, s, s, P)

                def group(i, r, ahead):
                    for j in range(4):
                        placed(i, j, 4 * i + j, j)
                        product(1, 4 * i + (j + 4), j, P)
                        if j >= 1:
                            weigh(4 * i + (j - 1), j - 1)
                        if ahead:
                            onehots(i + 1, 1 - r, range(2 * j, 2 * j + 2))
                    weigh(4 * i + 3, 3)

                group(0, 0, True)
                group(1, 1, True)
                group(2, 0, True)
                group(3, 1, False)

            def experts2():
                for s in range(2):
                    product(2, s, s, P)
                with dve.Fori(0, 4) as i:
                    for j in range(2):
                        dve.wait_ge(S(f"gb_in{j}"), 16 * (2 * i + (GB0[2] + 2)))
                        for s in range(2):
                            product(2, 4 * i + (2 * j + s + 2), s, P, gate=gb[:, j, s * 512:(s + 1) * 512])

            def experts3():
                with dve.Fori(0, 4) as i:
                    for j in range(2):
                        gate_tokens(3, i, j)
                        for s in range(6):
                            product(3, 12 * i + (6 * j + s), s, F3_M[s % 3])

            def add_out(layer):
                for c in range(2):
                    dve.wait_ge(S("f_out"), 2 * layer + c + 1)
                    ins = dve.tensor_tensor(x[:, 4 * c:4 * c + 4, :], bank[c][:, :].rearrange("p (t d) -> p t d", t=4),
                                            x[:, 4 * c:4 * c + 4, :], ALU.add)
                    chain(ins)

            for name in ("at_lg", "at_xn", "at_xT", "at_xTc", "at_p", "at_res", "at_on", "at_ot", "at_otc",
                         "gates_used0", "gates_used1", "gates_used3", "h1", "h2", "h3",
                         "down1", "down2", "down3", "scattered"):
                dve.sem_inc(S(name), CREDIT)
            dve.sem_inc(S("gu0"), 2 * UPS[0])
            dve.sem_inc(S("gu3"), 2 * UPS[3])
            for name in ("at_ptc", "h0", "down0"):
                dve.sem_inc(S(name), 4)
            dve.sem_inc(S("xgc"), 1)
            dve.sem_inc(S("eo"), 1)
            dve.wait_ge(S("const"), 1)
            setup()
            dve.wait_ge(S("x_in"), 16)
            for layer in range(4):
                if layer in attn_layers:
                    if layer == 1:
                        value_bias()
                    stats(2 * layer)
                    attention(layer)
                    dve.sem_inc(S("attn_done"), 1)
                    dve.sem_inc(S("banks_free_a"), 1)
                if layer in route_layers():
                    stats(2 * layer + 1)
                    route(layer)
                    [experts0, experts1, experts2, experts3][layer]()
                    add_out(layer)
                    dve.sem_inc(S("banks_free"), 1)
            dve.sem_inc(S("final"), 1)
        return


def kernel(**inputs):
    import numpy as _np
    import concourse.bacc as _bacc
    from concourse import mybir as _mybir
    from concourse.bass_utils import run_bass_kernel_spmd as _run

    g = {k: _np.asarray(v) for k, v in inputs.items()}

    def chunks(w):
        return w.reshape(-1, 128, w.shape[-1]).transpose(1, 0, 2)

    def heads(w):
        return w.transpose(1, 0, 2).reshape(128, 8, 128)

    def up3(w):
        return w.transpose(0, 2, 1)

    def down3(w, rows=128):
        return w.reshape(w.shape[0], -1, rows, 128).transpose(0, 2, 1, 3)

    f3d = _np.zeros((8, 3, 128, 128), _np.float32)
    f3d.reshape(8, 384, 128)[:, 0:352] = up3(g["L3_ffn_down_w"])
    pairs = lambda w: w.reshape(8, 2, 128, 64).transpose(0, 2, 1, 3).reshape(8, 128, 128)
    arrays = {
        "x_in": g["x"].reshape(1024, 128),
        "ctxT": g["ctx_1024"].reshape(256, 128).T,
        "fside": g["fside_SxS2_0"],
        "qmask": g["mask_BxS_bf1"].view(_np.uint8).reshape(8, 128).T,
        "aw0": _np.stack([g["L0_xattn_Wq"], g["L0_xattn_Wk"].T, g["L0_xattn_Wv"].T, g["L0_xattn_Wo"].T], 1),
        "aw1": chunks(g["L1_xattn_fc_w"].T),
        "fmT": _np.tile(_np.concatenate([g["L1_xattn_fm_w"].T, g["L1_xattn_fm_b"].reshape(8, 1)], 1), (16, 1)),
        "fmb": g["L1_xattn_fm_b"],
        "fcb": g["L1_xattn_fc_b"],
        "aw2": _np.stack([g["L2_xattn_W_q"], g["L2_xattn_W_k"].T, g["L2_xattn_W_v"].T, g["L2_xattn_W_o"].T], 1),
        "aw3": _np.stack([chunks(g["L3_xattn_Wq"].transpose(0, 2, 1).reshape(1024, 128)), heads(g["L3_xattn_Wk"]),
                          heads(g["L3_xattn_Wv"]), chunks(g["L3_xattn_Wo"])], 1),
        "wr0": g["L0_ffn_Wr"],
        "wr1": g["L1_ffn_gate_w"].T,
        "wr2": g["L2_ffn_Wr"],
        "wr3": g["L3_ffn_router_w"].T,
        "fw0": _np.concatenate([g["L0_ffn_W1"], down3(g["L0_ffn_W2"]).reshape(8, 128, 512)], 2),
        "fw1": _np.concatenate([up3(g["L1_ffn_Wg"]), up3(g["L1_ffn_Wu"]),
                                down3(up3(g["L1_ffn_Wd"])).reshape(16, 128, 512)], 2),
        "fw2": _np.concatenate([pairs(g["L2_ffn_Wg"]), pairs(g["L2_ffn_Wu"]), g["L2_ffn_Wd"].reshape(8, 128, 128)], 2),
        "fw3": _np.concatenate([up3(g["L3_ffn_gate_w"]), up3(g["L3_ffn_up_w"]),
                                f3d.transpose(0, 2, 1, 3).reshape(8, 128, 384)], 2),
        "sh1": _np.concatenate([g["L1_ffn_Sg"].T.reshape(128, 2, 128), g["L1_ffn_Su"].T.reshape(128, 2, 128),
                                chunks(g["L1_ffn_Sd"].T)], 1),
        "sh2": _np.stack([g["L2_ffn_Sg"], g["L2_ffn_Su"], g["L2_ffn_Sd"]], 1),
    }
    nc = _bacc.Bacc("TRN2", target_bir_lowering=False, num_devices=1)
    feeds, args = {}, []
    for name, a in arrays.items():
        a = _np.ascontiguousarray(a)
        feeds[f"in_{name}"] = a
        args.append(nc.dram_tensor(f"in_{name}", a.shape, _mybir.dt.from_np(a.dtype), kind="ExternalInput").ap())
    result = nc.dram_tensor("result", (1024, 128), _mybir.dt.float32, kind="ExternalOutput").ap()
    build(nc, *args, result)
    r = _run(nc, [feeds], core_ids=[0])
    return r.results[0]["result"].reshape(4, 256, 128)
```
